# Optimizing a Trainium2 kernel written in Bass

```python
import numpy as np
import jax
import jax.numpy as jnp

def _softmax(x, axis=-1):
    return jax.nn.softmax(x, axis=axis)

def _gelu(x):
    return jax.nn.gelu(x, approximate=True)

def _silu(x):
    return jax.nn.silu(x)

def _sigmoid(x):
    return jax.nn.sigmoid(x)

def _layernorm(x, axis=-1, eps=1e-05):
    m = jnp.mean(x, axis=axis, keepdims=True)
    v = jnp.var(x, axis=axis, keepdims=True)
    return (x - m) / jnp.sqrt(v + eps)

def _scatter_add(tgt, idx, src, axis=0):
    return tgt.at[idx].add(src)

def _segment_sum(src, seg, n):
    return jax.ops.segment_sum(src, seg, n)
kernel_name = 'mk_sandwich_d1_jaxref_r8_02f88b'

def setup_inputs(seed: int=0):
    np.random.seed(seed)
    _w = jnp.asarray

    def _L0_attn_setup():
        import jax, jax.numpy as jnp
        import numpy as np
        DIM = 128
        D_INNER = 128
        N_STATE = 32
        N_BLOCKS = 4
        TOP_K = 2
        ROUTER_TEMP = 1.0
        INIT_BETA_BIAS = 2.0
        BATCH = 16
        T = 256

        def _xavier(key, shape):
            fan_out, fan_in = shape
            lim = jnp.sqrt(6.0 / (fan_in + fan_out))
            return jax.random.uniform(key, shape, jnp.float32, -lim, lim)

        def _cell_scan(x_rnn, W_router, W_kv, W_beta, b_beta, W_q):
            Tt, batch, D = x_rnn.shape
            n, nb = (N_STATE, N_BLOCKS)
            xf = x_rnn.reshape(Tt * batch, D)
            logits = (xf @ W_router.T).reshape(Tt, batch, nb) / ROUTER_TEMP
            kv = (xf @ W_kv.T).reshape(Tt, batch, nb, 2, n)
            beta = jax.nn.sigmoid((xf @ W_beta.T).reshape(Tt, batch, nb, n) + b_beta)
            q = (xf @ W_q.T).reshape(Tt, batch, n)
            S0 = jnp.zeros((batch, nb, n, n), x_rnn.dtype)
            rows = jnp.arange(batch)[:, None]

            def step(S, inp):
                logits_t, k_t, v_t, beta_t, q_t = inp
                _, idx = jax.lax.top_k(logits_t, TOP_K)
                mask = jnp.zeros_like(logits_t).at[rows, idx].set(1.0)
                sm = jax.nn.softmax(logits_t, axis=-1)
                uw = mask * sm
                uw = uw / (uw.sum(-1, keepdims=True) + 1e-08)
                kn = k_t / (jnp.linalg.norm(k_t, axis=-1, keepdims=True) + 1e-06)
                retrieved = jnp.einsum('bnij,bnj->bni', S, kn)
                delta = v_t - retrieved
                outer = delta[..., :, None] * kn[..., None, :]
                S_upd = jnp.tanh(beta_t[..., None] * S + outer)
                w = uw[..., None, None]
                S_new = (1.0 - w) * S + w * S_upd
                Sq = jnp.einsum('bnij,bj->bni', S_new, q_t)
                block_out = Sq * (Sq * jax.nn.sigmoid(Sq))
                out_t = jnp.einsum('bn,bnd->bd', sm, block_out)
                return (S_new, out_t)
            S_final, outs = jax.lax.scan(step, S0, (logits, kv[..., 0, :], kv[..., 1, :], beta, q))
            return (outs, S_final)

        def _reference_tuple_inner(x, W_in, W_router, W_kv, W_beta, b_beta, W_q, W_out):
            x_proj = jax.nn.silu(x @ W_in.T)
            x_rnn = jnp.transpose(x_proj, (1, 0, 2))
            cell_out, S_final = _cell_scan(x_rnn, W_router, W_kv, W_beta, b_beta, W_q)
            y = jnp.transpose(cell_out, (1, 0, 2)) @ W_out.T
            return (y, S_final)
        key = jax.random.key(seed)
        ks = jax.random.split(key, 7)
        x = jax.random.normal(ks[0], (BATCH, T, DIM), jnp.float32)
        W_in = _xavier(ks[1], (D_INNER, DIM))
        W_router = _xavier(ks[2], (N_BLOCKS, D_INNER))
        W_kv = _xavier(ks[3], (N_BLOCKS * 2 * N_STATE, D_INNER))
        W_beta = _xavier(ks[4], (N_BLOCKS * N_STATE, D_INNER))
        b_beta = jnp.full((N_BLOCKS, N_STATE), INIT_BETA_BIAS, jnp.float32)
        W_q = _xavier(ks[5], (N_STATE, D_INNER))
        W_out = _xavier(ks[6], (DIM, N_STATE))
        return {'x': x, 'W_in': W_in, 'W_router': W_router, 'W_kv': W_kv, 'W_beta': W_beta, 'b_beta': b_beta, 'W_q': W_q, 'W_out': W_out}
    _L0_attn_in = _L0_attn_setup()

    def _L0_ffn_setup():
        import jax, jax.numpy as jnp
        import numpy as np
        D_IN, D_HID = (128, 512)

        def _ternary(key, shape):
            return jax.random.randint(key, shape, -1, 2).astype(jnp.float32)

        def _tlin(x, w, s):
            return jnp.einsum('bsi,oi->bso', x, w) * s
        key = jax.random.key(seed)
        ks = jax.random.split(key, 12)
        inv = lambda fan: 1.0 / np.sqrt(fan).astype(np.float32)
        return {'x': jax.random.normal(ks[0], (4, 256, D_IN), dtype=jnp.float32), 'w1_w': _ternary(ks[1], (D_HID, D_IN)), 'w1_s': jax.random.uniform(ks[2], (D_HID,), dtype=jnp.float32) * inv(D_IN), 'w2_w': _ternary(ks[3], (D_HID, D_IN)), 'w2_s': jax.random.uniform(ks[4], (D_HID,), dtype=jnp.float32) * inv(D_IN), 'h1_w': _ternary(ks[5], (D_HID, D_HID)), 'h1_s': jax.random.uniform(ks[6], (D_HID,), dtype=jnp.float32) * inv(D_HID), 'h2_w': _ternary(ks[7], (D_HID, D_HID)), 'h2_s': jax.random.uniform(ks[8], (D_HID,), dtype=jnp.float32) * inv(D_HID), 'w3_w': _ternary(ks[9], (D_IN, D_HID)), 'w3_s': jax.random.uniform(ks[10], (D_IN,), dtype=jnp.float32) * inv(D_HID)}
    _L0_ffn_in = _L0_ffn_setup()
    _d = {'L0_attn_x': _L0_attn_in['x'], 'L0_attn_W_in': _L0_attn_in['W_in'], 'L0_attn_W_router': _L0_attn_in['W_router'], 'L0_attn_W_kv': _L0_attn_in['W_kv'], 'L0_attn_W_beta': _L0_attn_in['W_beta'], 'L0_attn_b_beta': _L0_attn_in['b_beta'], 'L0_attn_W_q': _L0_attn_in['W_q'], 'L0_attn_W_out': _L0_attn_in['W_out'], 'L0_ffn_w1_w': _L0_ffn_in['w1_w'], 'L0_ffn_w1_s': _L0_ffn_in['w1_s'], 'L0_ffn_w2_w': _L0_ffn_in['w2_w'], 'L0_ffn_w2_s': _L0_ffn_in['w2_s'], 'L0_ffn_h1_w': _L0_ffn_in['h1_w'], 'L0_ffn_h1_s': _L0_ffn_in['h1_s'], 'L0_ffn_h2_w': _L0_ffn_in['h2_w'], 'L0_ffn_h2_s': _L0_ffn_in['h2_s'], 'L0_ffn_w3_w': _L0_ffn_in['w3_w'], 'L0_ffn_w3_s': _L0_ffn_in['w3_s']}
    _x0 = _d['L0_attn_x']
    _d['L0_attn_x'] = jax.random.normal(jax.random.fold_in(jax.random.key(seed), 1), (8, 512, 128), dtype=_x0.dtype)
    del _x0
    return _d

def reference(L0_attn_x, L0_attn_W_in, L0_attn_W_router, L0_attn_W_kv, L0_attn_W_beta, L0_attn_b_beta, L0_attn_W_q, L0_attn_W_out, L0_ffn_w1_w, L0_ffn_w1_s, L0_ffn_w2_w, L0_ffn_w2_s, L0_ffn_h1_w, L0_ffn_h1_s, L0_ffn_h2_w, L0_ffn_h2_s, L0_ffn_w3_w, L0_ffn_w3_s):

    def _L0_attn_ref(x, W_in, W_router, W_kv, W_beta, b_beta, W_q, W_out):
        import jax, jax.numpy as jnp
        import numpy as np
        DIM = 128
        D_INNER = 128
        N_STATE = 32
        N_BLOCKS = 4
        TOP_K = 2
        ROUTER_TEMP = 1.0
        INIT_BETA_BIAS = 2.0
        BATCH = 16
        T = 256

        def _xavier(key, shape):
            fan_out, fan_in = shape
            lim = jnp.sqrt(6.0 / (fan_in + fan_out))
            return jax.random.uniform(key, shape, jnp.float32, -lim, lim)

        def _cell_scan(x_rnn, W_router, W_kv, W_beta, b_beta, W_q):
            Tt, batch, D = x_rnn.shape
            n, nb = (N_STATE, N_BLOCKS)
            xf = x_rnn.reshape(Tt * batch, D)
            logits = (xf @ W_router.T).reshape(Tt, batch, nb) / ROUTER_TEMP
            kv = (xf @ W_kv.T).reshape(Tt, batch, nb, 2, n)
            beta = jax.nn.sigmoid((xf @ W_beta.T).reshape(Tt, batch, nb, n) + b_beta)
            q = (xf @ W_q.T).reshape(Tt, batch, n)
            S0 = jnp.zeros((batch, nb, n, n), x_rnn.dtype)
            rows = jnp.arange(batch)[:, None]

            def step(S, inp):
                logits_t, k_t, v_t, beta_t, q_t = inp
                _, idx = jax.lax.top_k(logits_t, TOP_K)
                mask = jnp.zeros_like(logits_t).at[rows, idx].set(1.0)
                sm = jax.nn.softmax(logits_t, axis=-1)
                uw = mask * sm
                uw = uw / (uw.sum(-1, keepdims=True) + 1e-08)
                kn = k_t / (jnp.linalg.norm(k_t, axis=-1, keepdims=True) + 1e-06)
                retrieved = jnp.einsum('bnij,bnj->bni', S, kn)
                delta = v_t - retrieved
                outer = delta[..., :, None] * kn[..., None, :]
                S_upd = jnp.tanh(beta_t[..., None] * S + outer)
                w = uw[..., None, None]
                S_new = (1.0 - w) * S + w * S_upd
                Sq = jnp.einsum('bnij,bj->bni', S_new, q_t)
                block_out = Sq * (Sq * jax.nn.sigmoid(Sq))
                out_t = jnp.einsum('bn,bnd->bd', sm, block_out)
                return (S_new, out_t)
            S_final, outs = jax.lax.scan(step, S0, (logits, kv[..., 0, :], kv[..., 1, :], beta, q))
            return (outs, S_final)

        def _reference_tuple_inner(x, W_in, W_router, W_kv, W_beta, b_beta, W_q, W_out):
            x_proj = jax.nn.silu(x @ W_in.T)
            x_rnn = jnp.transpose(x_proj, (1, 0, 2))
            cell_out, S_final = _cell_scan(x_rnn, W_router, W_kv, W_beta, b_beta, W_q)
            y = jnp.transpose(cell_out, (1, 0, 2)) @ W_out.T
            return (y, S_final)
        return _reference_tuple_inner(x, W_in, W_router, W_kv, W_beta, b_beta, W_q, W_out)[0]

    def _L0_ffn_ref(x, w1_w, w1_s, w2_w, w2_s, h1_w, h1_s, h2_w, h2_s, w3_w, w3_s):
        import jax, jax.numpy as jnp
        import numpy as np
        D_IN, D_HID = (128, 512)

        def _ternary(key, shape):
            return jax.random.randint(key, shape, -1, 2).astype(jnp.float32)

        def _tlin(x, w, s):
            return jnp.einsum('bsi,oi->bso', x, w) * s
        h = jax.nn.silu(_tlin(x, w1_w, w1_s)) * _tlin(x, w2_w, w2_s)
        h = jax.nn.gelu(_tlin(h, h1_w, h1_s), approximate=False)
        h = jax.nn.gelu(_tlin(h, h2_w, h2_s), approximate=False)
        return _tlin(h, w3_w, w3_s)
    x = L0_attn_x
    x = x + _layernorm(_L0_attn_ref(_layernorm(x, axis=-1), L0_attn_W_in, L0_attn_W_router, L0_attn_W_kv, L0_attn_W_beta, L0_attn_b_beta, L0_attn_W_q, L0_attn_W_out), axis=-1)
    x = x + _layernorm(_L0_ffn_ref(_layernorm(x, axis=-1), L0_ffn_w1_w, L0_ffn_w1_s, L0_ffn_w2_w, L0_ffn_w2_s, L0_ffn_h1_w, L0_ffn_h1_s, L0_ffn_h2_w, L0_ffn_h2_s, L0_ffn_w3_w, L0_ffn_w3_s), axis=-1)
    return x

_drawn_inputs = setup_inputs


def setup_inputs(seed=0):
    import zlib

    import numpy as np

    out = dict(_drawn_inputs(seed))
    spreads = {'L0_attn_b_beta': (2.0, 0.2)}
    factors = {}
    for name, (base, spread) in spreads.items():
        noise = np.random.default_rng([zlib.crc32(name.encode()), seed]).standard_normal(out[name].shape)
        drawn = base * np.exp(spread * noise) if base else spread * noise
        out[name] = jnp.asarray(drawn.astype(out[name].dtype))
    for name, factor in factors.items():
        out[name] = (out[name] * factor).astype(out[name].dtype)
    return out
```

```python
import concourse.bass as bass
from concourse import mybir
from contextlib import ExitStack

F32 = mybir.dt.float32
ALU = mybir.AluOpType
ACT = mybir.ActivationFunctionType
AX = mybir.AxisListType




class Count:

    def __init__(self, eng, sem, per_turn, base=0):
        self.eng, self.sem, self.per_turn, self.base, self.n = eng, sem, per_turn, base, 0

    def inc(self, ins):
        self.n += 1
        ins.then_inc(self.sem, 1)

    def wait(self, turn):
        self.eng.wait_ge(self.sem, turn * self.per_turn + (self.base + self.n))

    def close(self):
        assert self.n == self.per_turn, (self.n, self.per_turn)


def sandwich(nc, x, W_inT, W_kqrT, W_vT, W_betaT, b_beta, W_out_rows, w1T, w2T, h1T, h2T, w3T,
             w1_s, w2_s, h1_s, h2_s, w3_s, ident_in, out):
    B, T, D = x.shape
    P = 128
    NB = 4
    N = 32
    IG = P // (B * NB)
    NI = N // IG
    HI = NI // 2
    TQ = T // P
    KQ = NB * N + N + NB
    CH = 64
    GR = 32
    NG = T // GR
    HID = w1T.shape[1]
    MH = HID // P
    EPS = 1e-5

    with ExitStack() as ctx:
        def sb(name, shape):
            return ctx.enter_context(nc.sbuf_tensor(name, shape, F32))

        def sem(name):
            return ctx.enter_context(nc.semaphore(name))

        kn_d = nc.dram_tensor("kn_scratch", (B, NB, T, N), F32, kind="Internal").ap()
        q_d = nc.dram_tensor("q_scratch", (B, T, N), F32, kind="Internal").ap()
        v_d = nc.dram_tensor("v_scratch", (B, P, T), F32, kind="Internal").ap()
        beta_d = nc.dram_tensor("beta_scratch", (B, P, T), F32, kind="Internal").ap()
        r_d = nc.dram_tensor("router_scratch", (B, 3 * NB, T), F32, kind="Internal").ap()

        ident = sb("ident", [P, P])
        w_in = sb("w_in", [P, P])
        w_kqr = sb("w_kqr", [P, KQ])
        w_v = sb("w_v", [P, P])
        w_beta = sb("w_beta", [P, P])
        bb = sb("bb", [P, 1])
        w1 = sb("w1", [P, HID])
        w2 = sb("w2", [P, HID])
        h1 = sb("h1", [P, MH, HID])
        h2 = sb("h2", [P, MH, HID])
        w3 = sb("w3", [P, MH, D])
        s1 = sb("s1", [P, MH])
        s2 = sb("s2", [P, MH])
        sh1 = sb("sh1", [P, MH])
        sh2 = sb("sh2", [P, MH])
        s3 = sb("s3", [P, D])
        s12 = sb("s12", [P, MH])
        s1_half = sb("s1_half", [P, MH])
        bb_half = sb("bb_half", [P, 1])
        gate_v = sb("gate_v", [P, 1])
        gate_p = sb("gate_p", [P, 1])
        minus_half = sb("minus_half", [P, 16])
        plus_half = sb("plus_half", [P, 16])

        v_all = sb("v_all", [P, NI, T])
        beta_all = sb("beta_all", [P, NI, T])
        r_all = sb("r_all", [P, 3, T])
        bo = sb("bo", [P, NI, T])

        REG = 27424
        region = sb("region", [P, REG])
        taken = [0]

        def carve(*shape):
            n = 1
            for s in shape:
                n *= s
            a = region[:, taken[0]:taken[0] + n]
            taken[0] += n
            assert taken[0] <= REG
            if len(shape) == 1:
                return a
            names = "abcd"[:len(shape)]
            return a.rearrange(f"p ({' '.join(names)}) -> p {' '.join(names)}", **dict(zip(names, shape)))

        x_in = carve(TQ, D)
        xn = carve(TQ, D)
        xnT = carve(T)
        sg = carve(T)
        xpT = carve(T)
        v_st = carve(T)
        beta_st = carve(T)
        kq_st = carve(TQ, KQ)
        ksq = carve(TQ, NB * N)
        kn_st = carve(TQ, NB, N)
        stats = carve(TQ, 6)
        mv = carve(TQ, 2)
        var_eps = carve(TQ)
        rstd = carve(TQ)
        ss = carve(TQ * NB)
        nrm = carve(TQ * NB)
        nrm_eps = carve(TQ * NB)
        rnrm = carve(TQ * NB)
        lmax = carve(TQ)
        ld = carve(TQ, NB)
        beta_th = carve(T)
        lexp = carve(TQ, NB)
        lsum = carve(TQ)
        lsrec = carve(TQ)
        ge = carve(TQ, NB)
        wins = carve(TQ, NB)
        wins2 = carve(TQ, NB)
        mask = carve(TQ, NB)
        uw = carve(TQ, NB)
        usum = carve(TQ)
        usum_e = carve(TQ)
        urec = carve(TQ)
        r_tok = carve(TQ, 3, NB)
        r_st = carve(T)
        taken[0] = 0
        kn_ring = carve(2, CH, N)
        q_ring = carve(2, CH, N)
        S = carve(2, NI, N)
        Pk = carve(NI, N)
        ret = carve(NI)
        delta = carve(NI)
        outer = carve(NI, N)
        bS = carve(NI, N)
        pre = carve(NI, N)
        U = carve(NI, N)
        G = carve(NI, N)
        Pq = [carve(N, GR, NI) for _ in range(2)]
        sq_sig = carve(GR, NI)
        sq_a = carve(GR, NI)
        sq_b = carve(GR, NI)
        taken[0] = 0
        xt = carve(B, D)
        yn = carve(B, D)
        x1 = carve(B, D)
        x1n = carve(B, D)
        x1nT = carve(B * CH)
        sgA = carve(2, B * CH)
        tA = carve(2, B * CH)
        u = carve(MH, B * CH)
        g1 = carve(MH, B * CH)
        g2 = carve(MH, B * CH)
        on = carve(B, D)
        o_st = carve(B, D)
        w_out = carve(NI, B, D)
        bo_c = carve(NI, CH)
        cst = carve(B, 6)
        cmv = carve(B, 2)
        cve = carve(B)
        crs = carve(B)

        PS = ctx.enter_context(nc.psum_tensor("PS", [P, 8, 512], F32))

        weights_in = sem("weights_in")
        w_out_zero = sem("w_out_zero")
        w_out_in = sem("w_out_in")
        consts_set = sem("consts_set")
        scaled = sem("scaled")
        x_loaded = sem("x_loaded")
        va = sem("va")
        var_ready = sem("var_ready")
        rstd_ready = sem("rstd_ready")
        xn_ready = sem("xn_ready")
        xnT_psum = sem("xnT_psum")
        xnT_ready = sem("xnT_ready")
        xp_psum = sem("xp_psum")
        sg_ready = sem("sg_ready")
        xp_ready = sem("xp_ready")
        v_psum = sem("v_psum")
        beta_psum = sem("beta_psum")
        kq_psum = sem("kq_psum")
        v_staged = sem("v_staged")
        beta_staged = sem("beta_staged")
        kq_staged = sem("kq_staged")
        ksq_ready = sem("ksq_ready")
        ss_ready = sem("ss_ready")
        nrm_ready = sem("nrm_ready")
        kn_staged = sem("kn_staged")
        ld_ready = sem("ld_ready")
        lexp_ready = sem("lexp_ready")
        beta_tanh = sem("beta_tanh")
        r_tok_ready = sem("r_tok_ready")
        r_psum = sem("r_psum")
        r_staged = sem("r_staged")
        stored = sem("stored")

        resident_in = sem("resident_in")
        ring_in = [sem(f"ring_in{h}") for h in range(2)]
        state0 = sem("state0")
        vb = [sem(f"vb{h}") for h in range(2)]
        blended = [sem(f"blended{h}") for h in range(2)]
        bS_ready = [sem(f"bS_ready{h}") for h in range(2)]
        pre_ready = [sem(f"pre_ready{h}") for h in range(2)]
        U_ready = [sem(f"U_ready{h}") for h in range(2)]
        G_ready = [sem(f"G_ready{h}") for h in range(2)]
        Pq_ready = sem("Pq_ready")
        sq_psum = sem("sq_psum")
        sq_sig_ready = sem("sq_sig_ready")
        sq_chain = sem("sq_chain")
        bo_ready = sem("bo_ready")

        xt_in = sem("xt_in")
        y_psum = sem("y_psum")
        bo_c_ready = sem("bo_c_ready")
        vc = sem("vc")
        cvar_ready = sem("cvar_ready")
        crs_ready = sem("crs_ready")
        x1n_ready = sem("x1n_ready")
        x1nT_psum = sem("x1nT_psum")
        x1nT_ready = sem("x1nT_ready")
        gate_psum = sem("gate_psum")
        up_psum = sem("up_psum")
        sgA_ready = sem("sgA_ready")
        u_ready = sem("u_ready")
        gelu_psum = sem("gelu_psum")
        gelu_ready = sem("gelu_ready")
        o_psum = sem("o_psum")
        o_staged = sem("o_staged")
        out_stored = sem("out_stored")

        N_WEIGHTS = 16
        STORES = 5
        block = ctx.enter_context(nc.Block())

        @block.sync
        def _(sync):
            for dst, src in ((ident[:, :], ident_in), (w_in[:, :], W_inT), (w_kqr[:, :], W_kqrT),
                             (w_v[:, :], W_vT), (w_beta[:, :], W_betaT), (bb[:, :], b_beta),
                             (w1[:, :], w1T), (w2[:, :], w2T),
                             (h1[:, :, :], h1T.rearrange("(m p) n -> p m n", p=P)),
                             (h2[:, :, :], h2T.rearrange("(m p) n -> p m n", p=P)),
                             (w3[:, :, :], w3T.rearrange("(m p) n -> p m n", p=P)),
                             (s1[:, :], w1_s), (s2[:, :], w2_s), (sh1[:, :], h1_s), (sh2[:, :], h2_s),
                             (s3[:, :], w3_s)):
                sync.dma_start(dst, src).then_inc(weights_in, 16)
            with sync.Fori(0, B) as b:
                sync.wait_ge(xn_ready, b)
                sync.dma_start(x_in, x[bass.ds(b, 1)].rearrange("o (q p) d -> p (o q) d", p=P)
                               ).then_inc(x_loaded, 16)
                sync.wait_ge(v_staged, b + 1)
                sync.dma_start(v_d[bass.ds(b, 1)].rearrange("o p t -> (o p) t"), v_st).then_inc(stored, 16)
                sync.wait_ge(beta_staged, b + 1)
                sync.dma_start(beta_d[bass.ds(b, 1)].rearrange("o p t -> (o p) t"), beta_st).then_inc(stored, 16)
                sync.wait_ge(kq_staged, b * 2 + 2)
                sync.dma_start(q_d[bass.ds(b, 1)].rearrange("o (q p) j -> p (o q) j", p=P),
                               kq_st[:, :, NB * N:NB * N + N]).then_inc(stored, 16)
                sync.wait_ge(kn_staged, b + 1)
                for q in range(TQ):
                    sync.dma_start(kn_d[bass.ds(b, 1), :, q * P:(q + 1) * P, :].rearrange("o n p j -> p (o n) j"),
                                   kn_st[:, q]).then_inc(stored, 16)
                sync.wait_ge(r_staged, b + 1)
                sync.dma_start(r_d[bass.ds(b, 1)].rearrange("o r t -> (o r) t"), r_st[0:3 * NB, :]).then_inc(stored, 16)
            sync.wait_ge(stored, 16 * (4 + TQ) * B)
            sync.dma_start(v_all[:, :, :].rearrange("p i t -> p (i t)"),
                           v_d.rearrange("b (g i) t -> (b g) (i t)", i=NI)).then_inc(resident_in, 16)
            sync.dma_start(beta_all[:, :, :].rearrange("p i t -> p (i t)"),
                           beta_d.rearrange("b (g i) t -> (b g) (i t)", i=NI)).then_inc(resident_in, 16)
            for k in range(3):
                for g in range(IG):
                    sync.dma_start(r_all[g:P:IG, k, :], r_d[:, k * NB:(k + 1) * NB, :]
                                   ).then_inc(resident_in, 16)
            def load_ring(t0, half):
                for g in range(IG):
                    sync.dma_start(kn_ring[g:P:IG, half].rearrange("p t j -> p (t j)"),
                                   kn_d[:, :, bass.ds(t0, CH), :].rearrange("b n t j -> (b n) (t j)")
                                   ).then_inc(ring_in[half], 16)
                for g in range(NB * IG):
                    sync.dma_start(q_ring[g:P:NB * IG, half].rearrange("p t j -> p (t j)"),
                                   q_d[:, bass.ds(t0, CH), :].rearrange("b t j -> b (t j)")
                                   ).then_inc(ring_in[half], 16)

            for half in range(2):
                load_ring(half * CH, half)
            with sync.Fori(1, T // (2 * CH)) as c2:
                for half in range(2):
                    sync.wait_ge(blended[1], c2 * (2 * CH) - (1 - half) * CH)
                    sync.wait_ge(Pq_ready, c2 * (2 * CH) - (1 - half) * CH)
                    load_ring(c2 * (2 * CH) + half * CH, half)
            sync.wait_ge(bo_ready, NG)
            sync.wait_ge(w_out_zero, 1)
            for b in range(B):
                sync.dma_start(w_out[b * NB * IG:(b + 1) * NB * IG, :, b, :],
                               W_out_rows.rearrange("r (c d) -> r c d", c=NI)).then_inc(w_out_in, 16)
            with sync.Fori(0, T // CH) as c:
                sync.wait_ge(out_stored, c * 16)
                sync.dma_start(xt[0:CH], x[:, bass.ds(c * CH, CH), :].rearrange("b t d -> t b d")).then_inc(xt_in, 16)
                sync.wait_ge(o_staged, c + 1)
                sync.dma_start(out[:, bass.ds(c * CH, CH), :].rearrange("b t d -> t b d"), o_st[0:CH]
                               ).then_inc(out_stored, 16)
            sync.wait_ge(out_stored, 16 * (T // CH))

        RING_LOADS = 16 * (IG + NB * IG)
        RESIDENT = 16 * (2 + 3 * IG)
        HALF = [slice(h * HI, (h + 1) * HI) for h in range(2)]

        @block.gpsimd
        def _(pool):
            nc.gpsimd.memset(minus_half[:, :], -0.5)
            nc.gpsimd.memset(plus_half[:, :], 0.5).then_inc(consts_set, 1)
            pool.wait_ge(consts_set, 1)
            with pool.Fori(0, B) as b:
                pool.wait_ge(var_ready, b + 1)
                nc.gpsimd.tensor_tensor(rstd, var_eps, minus_half[:, 0:TQ], ALU.pow).then_inc(rstd_ready, 1)
                pool.wait_ge(kq_staged, b * 2 + 2)
                nc.gpsimd.tensor_tensor(ksq, kq_st[:, :, 0:NB * N], kq_st[:, :, 0:NB * N], ALU.mult
                                        ).then_inc(ksq_ready, 1)
                pool.wait_ge(ss_ready, b + 1)
                nc.gpsimd.tensor_tensor(nrm, ss, plus_half[:, :], ALU.pow).then_inc(nrm_ready, 1)

            pool.wait_ge(resident_in, RESIDENT)
            pool.wait_ge(state0, 1)

            def beta_state(par, t):
                for h in range(2):
                    pool.wait_ge(blended[h], t)
                    nc.gpsimd.tensor_tensor(bS[:, HALF[h]], S[:, (par + 1) % 2, HALF[h]],
                                            beta_all[:, HALF[h], bass.ds(t, 1)].to_broadcast([P, HI, N]),
                                            ALU.mult).then_inc(bS_ready[h], 1)

            def state_q(par, slot, tg, t, buf, half):
                pool.wait_ge(blended[0], t + 1)
                pool.wait_ge(blended[1], t + 1)
                nc.gpsimd.tensor_tensor(
                    Pq[buf][:, :, bass.ds(tg, 1), :].rearrange("p j o i -> p (o i) j"), S[:, par],
                    q_ring[:, half, bass.ds(slot, 1), :].to_broadcast([P, NI, N]),
                    ALU.mult).then_inc(Pq_ready, 1)

            with pool.Fori(0, T // (2 * CH)) as c2:
                for half in range(2):
                    pool.wait_ge(ring_in[half], (c2 + 1) * RING_LOADS)
                    for gg in range(CH // GR):
                        buf = gg % 2
                        g = c2 * (2 * CH // GR) + (half * CH // GR + gg)
                        pool.wait_ge(sq_psum, g - 1 if half or gg else c2 * (2 * CH // GR))
                        nc.gpsimd.tensor_tensor(gate_p[:, :], minus_half[:, 0:1], plus_half[:, 0:1], ALU.mult)
                        with pool.Fori(0, GR // 2) as s:
                            for par in range(2):
                                tg = s * 2 + par
                                t = c2 * (2 * CH) + s * 2 + (half * CH + gg * GR + par)
                                beta_state(par, t)
                                state_q(par, s * 2 + (gg * GR + par), tg, t, buf, half)
            pool.wait_ge(bo_ready, NG)
            nc.gpsimd.memset(w_out[:, :, :, :].rearrange("p c b d -> p (c b d)"), 0.0).then_inc(w_out_zero, 1)
            with pool.Fori(0, T // CH) as c:
                for k in range(3):
                    pool.wait_ge(cvar_ready, c * 3 + k + 1)
                    nc.gpsimd.tensor_tensor(crs[0:CH], cve[0:CH], minus_half[0:CH, 0:B], ALU.pow
                                            ).then_inc(crs_ready, 1)

        @block.scalar
        def _(act):
            act.wait_ge(weights_in, 16 * N_WEIGHTS)
            with act.Fori(0, B) as b:
                act.wait_ge(xnT_psum, b + 1)
                nc.scalar.activation(xnT, PS[:, 0, :], ACT.Copy).then_inc(xnT_ready, 1)
                act.wait_ge(xp_psum, b + 1)
                nc.scalar.activation(sg, PS[:, 1, :], ACT.Tanh, scale=0.5).then_inc(sg_ready, 1)
                act.wait_ge(v_psum, b + 1)
                act.wait_ge(stored, b * (16 * (4 + TQ)))
                nc.scalar.activation(v_st, PS[:, 2, :], ACT.Copy, scale=0.5).then_inc(v_staged, 1)
                act.wait_ge(beta_psum, b + 1)
                nc.scalar.activation(beta_th, PS[:, 3, :], ACT.Tanh, bias=bb_half[:, 0:1], scale=0.25
                                     ).then_inc(beta_tanh, 1)
                act.wait_ge(kq_psum, b + 1)
                for k in range(2):
                    nc.scalar.activation(kq_st[:, 2 * k:2 * k + 2, :],
                                         PS[:, 4 + k, 0:2 * KQ].rearrange("p (q c) -> p q c", q=2),
                                         ACT.Copy, scale=0.5).then_inc(kq_staged, 1)
                act.wait_ge(ld_ready, b + 1)
                nc.scalar.activation(lexp, ld, ACT.Exp).then_inc(lexp_ready, 1)
                act.wait_ge(r_psum, b + 1)
                nc.scalar.activation(r_st[0:3 * NB, :], PS[0:3 * NB, 6, :], ACT.Copy).then_inc(r_staged, 1)

            act.wait_ge(resident_in, RESIDENT)
            act.wait_ge(state0, 1)

            def keep(par, t):
                for h in range(2):
                    act.wait_ge(state0, 1)
                    act.wait_ge(blended[h], t)
                    nc.scalar.activation(G[:, HALF[h]], S[:, (par + 1) % 2, HALF[h]], ACT.Copy,
                                         scale=r_all[:, 1, bass.ds(t, 1)]).then_inc(G_ready[h], 1)
                    act.wait_ge(pre_ready[h], t + 1)
                    nc.scalar.activation(U[:, HALF[h]], pre[:, HALF[h]], ACT.Tanh).then_inc(U_ready[h], 1)

            def sig_readout(g, bank):
                act.wait_ge(sq_psum, g + 1)
                act.wait_ge(bo_ready, g)
                nc.scalar.activation(sq_sig.rearrange("p t i -> p (t i)"), PS[:, bank, 0:GR * NI], ACT.Tanh, scale=0.5
                                     ).then_inc(sq_sig_ready, 1)

            def steps_act(t0, n):
                with act.Fori(0, n // 2) as s:
                    for par in range(2):
                        keep(par, t0 + s * 2 + par)

            steps_act(0, GR)
            with act.Fori(0, (NG - 2) // 2) as gp:
                for k in range(2):
                    t0 = gp * (2 * GR) + (k + 1) * GR
                    steps_act(t0, GR - 8)
                    sig_readout(gp * 2 + k, k)
                    steps_act(t0 + (GR - 8), 8)
            steps_act((NG - 1) * GR, GR - 8)
            sig_readout(NG - 2, 0)
            steps_act(NG * GR - 8, 8)
            sig_readout(NG - 1, 1)

            act.wait_ge(scaled, 1)
            with act.Fori(0, T // CH) as c:
                act.wait_ge(y_psum, c)
                act.wait_ge(bo_ready, NG)
                nc.scalar.activation(bo_c, bo[:, :, bass.ds(c * CH, CH)], ACT.Copy, scale=0.5).then_inc(bo_c_ready, 1)
                act.wait_ge(x1nT_psum, c + 1)
                nc.scalar.activation(x1nT, PS[:, 2, :], ACT.Copy).then_inc(x1nT_ready, 1)
                for m in range(MH):
                    act.wait_ge(gate_psum, c * MH + m + 1)
                    act.wait_ge(u_ready, c * MH + m - 1 if m else c * MH)
                    nc.scalar.activation(sgA[:, m % 2], PS[:, 3 + m % 2, :], ACT.Tanh,
                                         scale=s1_half[:, m:m + 1]).then_inc(sgA_ready, 1)
                for layer, scale, dst in ((0, sh1, g1), (1, sh2, g2)):
                    for m in range(MH):
                        act.wait_ge(gelu_psum, c * (2 * MH) + (layer * MH + m + 1))
                        nc.scalar.activation(dst[:, m], PS[:, 3 + m % 2, :], ACT.Gelu,
                                             scale=scale[:, m:m + 1]).then_inc(gelu_ready, 1)

        @block.vector
        def _(dve):
            dve.wait_ge(weights_in, 16 * N_WEIGHTS)
            sc = Count(dve, scaled, 1)
            nc.vector.tensor_scalar(s1_half[:, :], s1[:, :], 0.5, None, ALU.mult).then_inc(vc, 1)
            nc.vector.tensor_scalar(bb_half[:, :], bb[:, :], 0.5, None, ALU.mult)
            dve.wait_ge(vc, 1)
            nc.vector.tensor_tensor(s12[:, :], s1_half[:, :], s2[:, :], ALU.mult).then_inc(vc, 1)
            dve.wait_ge(vc, 2)
            for m in range(MH):
                nc.vector.tensor_scalar(h1[:, m], h1[:, m], s12[:, m:m + 1], None, ALU.mult)
                last = nc.vector.tensor_tensor(w3[:, m], w3[:, m], s3[:, :], ALU.mult)
            sc.inc(last)

            VA = 33
            with dve.Fori(0, B) as b:
                ch = Count(dve, va, VA)

                def link(ins):
                    ch.inc(ins)
                    ch.wait(b)

                dve.wait_ge(x_loaded, b * 16 + 16)
                for q in range(TQ):
                    ch.inc(nc.vector.bn_stats(stats[:, q], x_in[:, q]))
                ch.wait(b)
                nc.vector.memset(gate_v[:, :], 0.0)
                for q in range(TQ):
                    ch.inc(nc.vector.bn_aggr(mv[:, q], stats[:, q]))
                ch.wait(b)
                nc.vector.tensor_scalar(var_eps, mv[:, :, 1], EPS, None, ALU.add).then_inc(var_ready, 1)
                dve.wait_ge(rstd_ready, b + 1)
                dve.wait_ge(xnT_psum, b)
                for q in range(TQ):
                    last = nc.vector.tensor_scalar(xn[:, q], x_in[:, q], mv[:, q, 0:1], rstd[:, q:q + 1],
                                                   ALU.subtract, ALU.mult)
                last.then_inc(xn_ready, 1)
                dve.wait_ge(sg_ready, b + 1)
                nc.vector.scalar_tensor_tensor(out=xpT, in0=sg, scalar=1.0, in1=PS[:, 1, :], op0=ALU.add,
                                               op1=ALU.mult).then_inc(xp_ready, 1)
                dve.wait_ge(kq_staged, b * 2 + 2)
                lg = kq_st[:, :, NB * N + N:]
                link(nc.vector.tensor_reduce(lmax, lg, AX.X, ALU.max))
                nc.vector.tensor_tensor(ld, lg, lmax.unsqueeze(2).to_broadcast([P, TQ, NB]), ALU.subtract
                                        ).then_inc(ld_ready, 1)
                for n in range(NB):
                    link(nc.vector.memset(wins[:, :, n:n + 1], float(n)))
                for s in range(1, NB):
                    link(nc.vector.tensor_tensor(ge[:, :, 0:NB - s], lg[:, :, 0:NB - s], lg[:, :, s:NB], ALU.is_ge))
                    link(nc.vector.tensor_tensor(wins[:, :, 0:NB - s], wins[:, :, 0:NB - s], ge[:, :, 0:NB - s],
                                                 ALU.add))
                    link(nc.vector.tensor_tensor(wins[:, :, s:NB], wins[:, :, s:NB], ge[:, :, 0:NB - s],
                                                 ALU.subtract))
                link(nc.vector.tensor_scalar(mask, wins, float(NB - 2), None, ALU.is_ge))
                dve.wait_ge(lexp_ready, b + 1)
                link(nc.vector.tensor_reduce(lsum, lexp, AX.X, ALU.add))
                link(nc.vector.reciprocal(lsrec, lsum))
                dve.wait_ge(r_psum, b)
                link(nc.vector.tensor_tensor(r_tok[:, :, 2], lexp, lsrec.unsqueeze(2).to_broadcast([P, TQ, NB]),
                                             ALU.mult))
                link(nc.vector.tensor_tensor(uw, mask, r_tok[:, :, 2], ALU.mult))
                link(nc.vector.tensor_reduce(usum, uw, AX.X, ALU.add))
                link(nc.vector.tensor_scalar(usum_e, usum, 1e-8, None, ALU.add))
                link(nc.vector.reciprocal(urec, usum_e))
                link(nc.vector.tensor_tensor(r_tok[:, :, 0], uw, urec.unsqueeze(2).to_broadcast([P, TQ, NB]),
                                             ALU.mult))
                nc.vector.tensor_scalar(r_tok[:, :, 1], r_tok[:, :, 0], -1.0, 1.0, ALU.mult, ALU.add
                                        ).then_inc(r_tok_ready, 1)
                dve.wait_ge(stored, b * (16 * (4 + TQ)))
                dve.wait_ge(beta_tanh, b + 1)
                nc.vector.tensor_scalar(beta_st, beta_th, 0.5, 0.5, ALU.mult, ALU.add).then_inc(beta_staged, 1)
                dve.wait_ge(ksq_ready, b + 1)
                nc.vector.tensor_reduce(ss, ksq.rearrange("p q (n j) -> p (q n) j", j=N), AX.X, ALU.add
                                        ).then_inc(ss_ready, 1)
                dve.wait_ge(nrm_ready, b + 1)
                link(nc.vector.tensor_scalar(nrm_eps, nrm, 1e-6, None, ALU.add))
                link(nc.vector.reciprocal(rnrm, nrm_eps))
                dve.wait_ge(stored, b * (16 * (4 + TQ)))
                for q in range(TQ):
                    last = nc.vector.tensor_tensor(
                        kn_st[:, q], kq_st[:, q, 0:NB * N].rearrange("p (n j) -> p n j", j=N),
                        rnrm[:, q * NB:(q + 1) * NB].unsqueeze(2).to_broadcast([P, NB, N]), ALU.mult)
                last.then_inc(kn_staged, 1)
                ch.close()

            dve.wait_ge(stored, 16 * (4 + TQ) * B)
            nc.vector.memset(S[:, :, :, :].rearrange("p a i j -> p (a i j)"), 0.0).then_inc(state0, 1)
            dve.wait_ge(state0, 1)
            dve.wait_ge(resident_in, RESIDENT)
            VB = 4

            def half_step(par, slot, half, t, h):
                ch = Count(dve, vb[h], VB)

                def link(ins):
                    ch.inc(ins)
                    ch.wait(t)
                hs = HALF[h]
                kn = kn_ring[:, half, bass.ds(slot, 1), :].to_broadcast([P, HI, N])
                dve.wait_ge(blended[h], t)
                link(nc.vector.tensor_tensor(Pk[:, hs], S[:, (par + 1) % 2, hs], kn, ALU.mult))
                link(nc.vector.tensor_reduce(ret[:, hs], Pk[:, hs], AX.X, ALU.add))
                link(nc.vector.tensor_tensor(delta[:, hs].unsqueeze(2), v_all[:, hs, bass.ds(t, 1)],
                                             ret[:, hs].unsqueeze(2), ALU.subtract))
                link(nc.vector.tensor_tensor(outer[:, hs], delta[:, hs].unsqueeze(2).to_broadcast([P, HI, N]), kn,
                                             ALU.mult))
                dve.wait_ge(bS_ready[h], t + 1)
                nc.vector.tensor_tensor(pre[:, hs], bS[:, hs], outer[:, hs], ALU.add).then_inc(pre_ready[h], 1)
                ch.close()

            def blend(par, t, h, first):
                hs = HALF[h]
                dve.wait_ge(U_ready[h], t + 1)
                dve.wait_ge(G_ready[h], t + 1)
                if not first:
                    dve.wait_ge(Pq_ready, t - 1)
                nc.vector.scalar_tensor_tensor(out=S[:, par, hs], in0=U[:, hs], scalar=r_all[:, 0, bass.ds(t, 1)],
                                               in1=G[:, hs], op0=ALU.mult, op1=ALU.add).then_inc(blended[h], 1)

            def steps(t0, slot0, half, n, peel=False):
                if peel:
                    for t in range(2):
                        for h in range(2):
                            half_step(t, t, 0, t, h)
                        for h in range(2):
                            blend(t, t, h, True)
                with dve.Fori(1 if peel else 0, n // 2) as s:
                    for par in range(2):
                        t = t0 + s * 2 + par
                        for h in range(2):
                            half_step(par, s * 2 + (slot0 + par), half, t, h)
                        for h in range(2):
                            blend(par, t, h, False)

            def readout(g, bank):
                pv = PS[:, bank, 0:GR * NI].rearrange("p (t i) -> p t i", i=NI)
                dve.wait_ge(sq_sig_ready, g + 1)
                nc.vector.scalar_tensor_tensor(out=sq_a, in0=sq_sig, scalar=1.0, in1=pv, op0=ALU.add, op1=ALU.mult
                                               ).then_inc(sq_chain, 1)
                dve.wait_ge(sq_chain, g * 2 + 1)
                nc.vector.tensor_tensor(sq_b, sq_a, pv, ALU.mult).then_inc(sq_chain, 1)
                dve.wait_ge(sq_chain, g * 2 + 2)
                nc.vector.tensor_tensor(bo[:, :, bass.ds(g * GR, GR)].rearrange("p i t -> p t i"), sq_b,
                                        r_all[:, 2, bass.ds(g * GR, GR)].unsqueeze(2).to_broadcast([P, GR, NI]),
                                        ALU.mult).then_inc(bo_ready, 1)

            def group(c2, k, peel=False):
                half, gg = k // 2, k % 2
                if gg == 0:
                    dve.wait_ge(ring_in[half], (c2 + 1) * RING_LOADS)
                    nc.vector.memset(gate_v[:, :], 0.0)
                t0 = c2 * (2 * CH) + k * GR
                steps(t0, gg * GR, half, GR - 8, peel)
                if not peel:
                    readout(c2 * 4 + (k - 1), (k - 1) % 2)
                steps(t0 + (GR - 8), gg * GR + GR - 8, half, 8)

            for k in range(4):
                group(0, k, peel=(k == 0))
            with dve.Fori(1, T // (2 * CH)) as c2:
                for k in range(4):
                    group(c2, k)
            readout(NG - 1, 1)

            VC = 34
            with dve.Fori(0, T // CH) as c:
                ch = Count(dve, vc, VC, base=2)

                def link2(ins):
                    ch.inc(ins)
                    ch.wait(c)

                def moments(src, k):
                    for b in range(B):
                        ch.inc(nc.vector.bn_stats(cst[0:CH, b], src[:, b]))
                    ch.wait(c)
                    nc.vector.memset(gate_v[:, :], 0.0)
                    for b in range(B):
                        last = nc.vector.bn_aggr(cmv[0:CH, b], cst[0:CH, b])
                    link2(last)
                    nc.vector.tensor_scalar(cve[0:CH], cmv[0:CH, :, 1], EPS, None, ALU.add).then_inc(cvar_ready, 1)
                    dve.wait_ge(crs_ready, c * 3 + k + 1)

                def normal(dst, src):
                    for b in range(B):
                        last = nc.vector.tensor_scalar(dst[0:CH, b], src[:, b], cmv[0:CH, b, 0:1],
                                                       crs[0:CH, b:b + 1], ALU.subtract, ALU.mult)
                    return last

                psY = PS[0:CH, 0:2, :].rearrange("p a (b d) -> p (a b) d", d=D)
                dve.wait_ge(y_psum, c + 1)
                dve.wait_ge(xt_in, c * 16 + 16)
                moments(psY, 0)
                link2(normal(yn, psY))
                link2(nc.vector.tensor_tensor(x1[0:CH], xt[0:CH], yn[0:CH], ALU.add))
                moments(x1[0:CH], 1)
                normal(x1n, x1[0:CH]).then_inc(x1n_ready, 1)
                for m in range(MH):
                    dve.wait_ge(sgA_ready, c * MH + m + 1)
                    link2(nc.vector.scalar_tensor_tensor(out=tA[:, m % 2], in0=sgA[:, m % 2], scalar=1.0,
                                                         in1=PS[:, 3 + m % 2, :], op0=ALU.add, op1=ALU.mult))
                    dve.wait_ge(up_psum, c * MH + m + 1)
                    nc.vector.tensor_tensor(u[:, m], tA[:, m % 2], PS[:, 5 + m % 2, :], ALU.mult).then_inc(u_ready, 1)
                dve.wait_ge(o_psum, c + 1)
                moments(psY, 2)
                link2(normal(on, psY))
                nc.vector.tensor_tensor(o_st[0:CH], x1[0:CH], on[0:CH], ALU.add).then_inc(o_staged, 1)
                ch.close()

        @block.tensor
        def _(pe):
            pe.wait_ge(weights_in, 16 * N_WEIGHTS)
            with pe.Fori(0, B) as b:
                pe.wait_ge(xn_ready, b + 1)
                for q in range(TQ):
                    last = nc.tensor.transpose(PS[:, 0, q * P:(q + 1) * P], xn[:, q], ident[:, :])
                last.then_inc(xnT_psum, 1)
                pe.wait_ge(xnT_ready, b + 1)
                nc.tensor.matmul(PS[:, 1, :], w_in[:, :], xnT, start=True, stop=True).then_inc(xp_psum, 1)
                pe.wait_ge(xp_ready, b + 1)
                nc.tensor.matmul(PS[:, 2, :], w_v[:, :], xpT, start=True, stop=True).then_inc(v_psum, 1)
                nc.tensor.matmul(PS[:, 3, :], w_beta[:, :], xpT, start=True, stop=True).then_inc(beta_psum, 1)
                for q in range(TQ):
                    last = nc.tensor.matmul(PS[:, 4 + q // 2, (q % 2) * KQ:(q % 2 + 1) * KQ],
                                            xpT[:, q * P:(q + 1) * P], w_kqr[:, :], start=(q % 2 == 0), stop=True,
                                            skip_group_check=True)
                last.then_inc(kq_psum, 1)
                pe.wait_ge(r_tok_ready, b + 1)
                for q in range(TQ):
                    last = nc.tensor.transpose(PS[0:3 * NB, 6, q * P:(q + 1) * P],
                                               r_tok[:, q].rearrange("p k n -> p (k n)"), ident[:, :])
                last.then_inc(r_psum, 1)

            pe.wait_ge(r_staged, B)
            with pe.Fori(0, NG // 2) as gp:
                for k in range(2):
                    pe.wait_ge(Pq_ready, gp * (2 * GR) + (k + 1) * GR)
                    pe.wait_ge(bo_ready, gp * 2 + k - 1 if k else gp * 2)
                    for j in range(N):
                        last = nc.tensor.matmul(PS[:, k, 0:GR * NI], ident[:, :],
                                                Pq[k][:, j].rearrange("p t i -> p (t i)"),
                                                start=(j == 0), stop=(j == N - 1))
                    last.then_inc(sq_psum, 1)

            pe.wait_ge(w_out_in, 16 * B)
            pe.wait_ge(bo_ready, NG)
            pe.wait_ge(scaled, 1)
            with pe.Fori(0, T // CH) as c:
                pe.wait_ge(bo_c_ready, c + 1)
                pe.wait_ge(o_staged, c)
                for a in range(2):
                    for i in range(NI):
                        last = nc.tensor.matmul(PS[0:CH, a, :], bo_c[:, i],
                                                w_out[:, i, a * B // 2:(a + 1) * B // 2, :].rearrange("p b d -> p (b d)"),
                                                start=(i == 0), stop=(i == NI - 1))
                last.then_inc(y_psum, 1)
                pe.wait_ge(scaled, 1)
                pe.wait_ge(x1n_ready, c + 1)
                for b in range(B):
                    last = nc.tensor.transpose(PS[:, 2, b * CH:(b + 1) * CH], x1n[0:CH, b], ident[0:CH, 0:CH])
                last.then_inc(x1nT_psum, 1)
                pe.wait_ge(x1nT_ready, c + 1)
                for m in range(MH):
                    if m >= 2:
                        pe.wait_ge(u_ready, c * MH + m - 1)
                    nc.tensor.matmul(PS[:, 3 + m % 2, :], w1[:, m * P:(m + 1) * P], x1nT, start=True, stop=True
                                     ).then_inc(gate_psum, 1)
                    nc.tensor.matmul(PS[:, 5 + m % 2, :], w2[:, m * P:(m + 1) * P], x1nT, start=True, stop=True
                                     ).then_inc(up_psum, 1)
                pe.wait_ge(u_ready, c * MH + MH)
                for layer, w, src in ((0, h1, u), (1, h2, g1)):
                    if layer:
                        pe.wait_ge(gelu_ready, c * (2 * MH) + MH)
                    for m in range(MH):
                        if m >= 2:
                            pe.wait_ge(gelu_ready, c * (2 * MH) + (layer * MH + m - 1))
                        for k in range(MH):
                            last = nc.tensor.matmul(PS[:, 3 + m % 2, :], w[:, k, m * P:(m + 1) * P], src[:, k],
                                                    start=(k == 0), stop=(k == MH - 1))
                        last.then_inc(gelu_psum, 1)
                pe.wait_ge(gelu_ready, c * (2 * MH) + 2 * MH)
                for b in range(B):
                    for k in range(MH):
                        last = nc.tensor.matmul(PS[0:CH, b // 4, (b % 4) * D:(b % 4 + 1) * D],
                                                g2[:, k, b * CH:(b + 1) * CH], w3[:, k],
                                                start=(k == 0), stop=(k == MH - 1))
                last.then_inc(o_psum, 1)


def kernel(L0_attn_x, L0_attn_W_in, L0_attn_W_router, L0_attn_W_kv, L0_attn_W_beta, L0_attn_b_beta,
           L0_attn_W_q, L0_attn_W_out, L0_ffn_w1_w, L0_ffn_w1_s, L0_ffn_w2_w, L0_ffn_w2_s, L0_ffn_h1_w,
           L0_ffn_h1_s, L0_ffn_h2_w, L0_ffn_h2_s, L0_ffn_w3_w, L0_ffn_w3_s):
    import numpy as np
    import concourse.bacc as bacc
    from concourse.bass_utils import run_bass_kernel_spmd

    D = L0_attn_x.shape[2]
    NB, N = L0_attn_b_beta.shape
    IG = 4
    kv = np.asarray(L0_attn_W_kv).reshape(NB, 2, N, D)
    W_k = kv[:, 0].reshape(NB * N, D)
    W_v = kv[:, 1].reshape(NB * N, D)

    def column(s):
        return np.asarray(s).reshape(-1, 128).T

    W_out_rows = np.asarray(L0_attn_W_out).T.reshape(IG, (N // IG) * D)
    arrays = {
        "x": L0_attn_x,
        "W_inT": np.asarray(L0_attn_W_in).T,
        "W_kqrT": np.concatenate([W_k, np.asarray(L0_attn_W_q), np.asarray(L0_attn_W_router)]).T,
        "W_vT": W_v.T,
        "W_betaT": np.asarray(L0_attn_W_beta).T,
        "b_beta": np.asarray(L0_attn_b_beta).reshape(NB * N, 1),
        "W_out_rows": np.tile(W_out_rows, (NB, 1)),
        "w1T": np.asarray(L0_ffn_w1_w).T,
        "w2T": np.asarray(L0_ffn_w2_w).T,
        "h1T": np.asarray(L0_ffn_h1_w).T,
        "h2T": np.asarray(L0_ffn_h2_w).T,
        "w3T": np.asarray(L0_ffn_w3_w).T,
        "w1_s": column(L0_ffn_w1_s),
        "w2_s": column(L0_ffn_w2_s),
        "h1_s": column(L0_ffn_h1_s),
        "h2_s": column(L0_ffn_h2_s),
        "w3_s": np.tile(np.asarray(L0_ffn_w3_s), (128, 1)),
        "ident_in": np.eye(128, dtype=np.float32),
    }
    nc = bacc.Bacc("TRN2", target_bir_lowering=False, num_devices=1)
    feeds, args = {}, []
    for name, a in arrays.items():
        a = np.ascontiguousarray(a)
        feeds[name + "_dram"] = a
        args.append(nc.dram_tensor(name + "_dram", a.shape, mybir.dt.from_np(a.dtype), kind="ExternalInput").ap())
    args.append(nc.dram_tensor("out_dram", np.asarray(L0_attn_x).shape, F32, kind="ExternalOutput").ap())
    sandwich(nc, *args)
    r = run_bass_kernel_spmd(nc, [feeds], core_ids=[0])
    return r.results[0]["out_dram"]
```

```python
import concourse.bass as bass
from concourse import mybir
from contextlib import ExitStack

F32 = mybir.dt.float32
ALU = mybir.AluOpType
ACT = mybir.ActivationFunctionType
AX = mybir.AxisListType




def some(count):
    return not isinstance(count, int) or count > 0


class Count:

    def __init__(self, eng, sem, per_turn, base=0):
        self.eng, self.sem, self.per_turn, self.base, self.n = eng, sem, per_turn, base, 0

    def inc(self, ins):
        self.n += 1
        ins.then_inc(self.sem, 1)

    def wait(self, turn):
        self.eng.wait_ge(self.sem, turn * self.per_turn + (self.base + self.n))

    def close(self):
        assert self.n == self.per_turn, (self.n, self.per_turn)


def sandwich(nc, x, W_inT, W_kqrT, W_vT, W_betaT, b_beta, W_out_rows, w1T, w2T, h1T, h2T, w3T,
             w1_s, w2_s, h1_s, h2_s, w3_s, ident_in, out):
    B, T, D = x.shape
    P = 128
    NB = 4
    N = 32
    IG = P // (B * NB)
    NI = N // IG
    HI = NI // 2
    TQ = T // P
    KQ = NB * N + N + NB
    CH = 32
    GR = CH // 2
    NC = T // CH
    BH = B // 4
    SR = 4
    HID = w1T.shape[1]
    MH = HID // P
    EPS = 1e-5

    with ExitStack() as ctx:
        def sb(name, shape):
            return ctx.enter_context(nc.sbuf_tensor(name, shape, F32))

        def sem(name):
            return ctx.enter_context(nc.semaphore(name))

        kn_d = nc.dram_tensor("kn_scratch", (B, NB, T, N), F32, kind="Internal").ap()
        q_d = nc.dram_tensor("q_scratch", (B, T, N), F32, kind="Internal").ap()
        v_d = nc.dram_tensor("v_scratch", (B, P, T), F32, kind="Internal").ap()
        beta_d = nc.dram_tensor("beta_scratch", (B, P, T), F32, kind="Internal").ap()
        r_d = nc.dram_tensor("router_scratch", (B, 3 * NB, T), F32, kind="Internal").ap()

        ident = sb("ident", [P, P])
        w_in = sb("w_in", [P, P])
        w_kqr = sb("w_kqr", [P, KQ])
        w_v = sb("w_v", [P, P])
        w_beta = sb("w_beta", [P, P])
        bb = sb("bb", [P, 1])
        w1 = sb("w1", [P, HID])
        w2 = sb("w2", [P, HID])
        h1 = sb("h1", [P, MH, HID])
        h2 = sb("h2", [P, MH, HID])
        w3 = sb("w3", [P, MH, D])
        s1 = sb("s1", [P, MH])
        s2 = sb("s2", [P, MH])
        sh1 = sb("sh1", [P, MH])
        sh2 = sb("sh2", [P, MH])
        s3 = sb("s3", [P, D])
        s12 = sb("s12", [P, MH])
        s1_half = sb("s1_half", [P, MH])
        bb_half = sb("bb_half", [P, 1])
        gate_v = sb("gate_v", [P, 1])
        gate_p = sb("gate_p", [P, 1])
        minus_half = sb("minus_half", [P, 16])
        plus_half = sb("plus_half", [P, 16])

        v_all = sb("v_all", [P, NI, T + GR])
        beta_all = sb("beta_all", [P, NI, T + GR])
        r_all = sb("r_all", [P, 3, T + GR])
        w_out = sb("w_out", [P, NI, B, D])

        REG = 28400
        region = sb("region", [P, REG])
        taken = [0]

        def carve(*shape):
            n = 1
            for s in shape:
                n *= s
            a = region[:, taken[0]:taken[0] + n]
            taken[0] += n
            assert taken[0] <= REG
            if len(shape) == 1:
                return a
            names = "abcd"[:len(shape)]
            return a.rearrange(f"p ({' '.join(names)}) -> p {' '.join(names)}", **dict(zip(names, shape)))

        x_in = carve(TQ, D)
        xn = carve(TQ, D)
        xnT = carve(T)
        sg = carve(T)
        xpT = carve(T)
        v_st = carve(T)
        beta_st = carve(T)
        kq_st = carve(TQ, KQ)
        ksq = carve(TQ, NB * N)
        kn_st = carve(TQ, NB, N)
        stats = carve(TQ, 6)
        mv = carve(TQ, 2)
        var_eps = carve(TQ)
        rstd = carve(TQ)
        ss = carve(TQ * NB)
        nrm = carve(TQ * NB)
        nrm_eps = carve(TQ * NB)
        rnrm = carve(TQ * NB)
        lmax = carve(TQ)
        ld = carve(TQ, NB)
        beta_th = carve(T)
        lexp = carve(TQ, NB)
        lsum = carve(TQ)
        lsrec = carve(TQ)
        ge = carve(TQ, NB)
        wins = carve(TQ, NB)
        wins2 = carve(TQ, NB)
        mask = carve(TQ, NB)
        uw = carve(TQ, NB)
        usum = carve(TQ)
        usum_e = carve(TQ)
        urec = carve(TQ)
        r_tok = carve(TQ, 3, NB)
        r_st = carve(T)
        taken[0] = 0
        kn_ring = carve(CH, N)
        q_ring = carve(CH, N)
        beta_ring = carve(NI, CH)
        w_ring = carve(2, CH)
        S = carve(SR, NI, N)
        Pk = carve(CH, NI, N + 1)
        delta = carve(NI)
        outer = carve(NI, N)
        bS = carve(NI, N)
        pre = carve(NI, N)
        U = carve(NI, N)
        G = carve(NI, N)
        Pq = [carve(N, GR, NI) for _ in range(2)]
        sq_th = carve(GR, NI)
        sq_a = carve(GR, NI)
        sq_b = carve(GR, NI)
        bo = carve(NI, CH)
        TK = B * CH
        xt = carve(BH, D)
        yn = carve(BH, D)
        x1 = carve(BH, D)
        x1_old = carve(BH, D)
        x1n = carve(BH, D)
        x1nT = carve(TK)
        gate_th = carve(2, TK)
        gate_t = carve(2, TK)
        u = carve(MH, TK)
        g1 = carve(MH, TK)
        g2 = u
        on = carve(BH, D)
        o_st = carve(BH, D)
        cst = carve(3, BH, 6)
        cmv = carve(3, BH, 2)
        cve = carve(3, BH)
        crs = carve(3, BH)

        PS = ctx.enter_context(nc.psum_tensor("PS", [P, 8, 512], F32))

        weights_in = sem("weights_in")
        w_out_zero = sem("w_out_zero")
        w_out_in = sem("w_out_in")
        consts_set = sem("consts_set")
        scaled = sem("scaled")
        x_loaded = sem("x_loaded")
        va = sem("va")
        var_ready = sem("var_ready")
        rstd_ready = sem("rstd_ready")
        xn_ready = sem("xn_ready")
        xnT_psum = sem("xnT_psum")
        xnT_ready = sem("xnT_ready")
        xp_psum = sem("xp_psum")
        sg_ready = sem("sg_ready")
        xp_ready = sem("xp_ready")
        v_psum = sem("v_psum")
        beta_psum = sem("beta_psum")
        kq_psum = sem("kq_psum")
        v_staged = sem("v_staged")
        beta_staged = sem("beta_staged")
        kq_staged = sem("kq_staged")
        ksq_ready = sem("ksq_ready")
        ss_ready = sem("ss_ready")
        nrm_ready = sem("nrm_ready")
        kn_staged = sem("kn_staged")
        ld_ready = sem("ld_ready")
        lexp_ready = sem("lexp_ready")
        beta_tanh = sem("beta_tanh")
        r_tok_ready = sem("r_tok_ready")
        r_psum = sem("r_psum")
        r_staged = sem("r_staged")
        stored = sem("stored")

        resident_in = sem("resident_in")
        padded = sem("padded")
        ring_in = [sem(f"ring_in{h}") for h in range(2)]
        filled = [sem(f"filled{h}") for h in range(2)]
        state0 = sem("state0")
        blended = [sem(f"blended{h}") for h in range(2)]
        Pk_ready = [sem(f"Pk_ready{h}") for h in range(2)]
        delta_ready = [sem(f"delta_ready{h}") for h in range(2)]
        outer_ready = [sem(f"outer_ready{h}") for h in range(2)]
        bS_ready = [sem(f"bS_ready{h}") for h in range(2)]
        pre_ready = [sem(f"pre_ready{h}") for h in range(2)]
        U_ready = [sem(f"U_ready{h}") for h in range(2)]
        G_ready = [sem(f"G_ready{h}") for h in range(2)]
        q_used = sem("q_used")
        sq_psum = [sem(f"sq_psum{h}") for h in range(2)]
        sq_tanh = [sem(f"sq_tanh{h}") for h in range(2)]
        sq_a_ready = [sem(f"sq_a_ready{h}") for h in range(2)]
        sq_b_ready = [sem(f"sq_b_ready{h}") for h in range(2)]
        bo_ready = [sem(f"bo_ready{h}") for h in range(2)]
        xt_in = sem("xt_in")
        y_psum = sem("y_psum")
        stats_ready = [sem(f"stats_ready{k}") for k in range(3)]
        aggr_ready = [sem(f"aggr_ready{k}") for k in range(3)]
        cvar_ready = [sem(f"cvar_ready{k}") for k in range(3)]
        crs_ready = [sem(f"crs_ready{k}") for k in range(3)]
        yn_ready = sem("yn_ready")
        x1_ready = sem("x1_ready")
        x1_saved = sem("x1_saved")
        x1n_ready = sem("x1n_ready")
        x1nT_psum = sem("x1nT_psum")
        x1nT_ready = sem("x1nT_ready")
        gate_psum = [sem(f"gate_psum{m}") for m in range(MH)]
        gate_tanh = [sem(f"gate_tanh{m}") for m in range(MH)]
        gate_ready = [sem(f"gate_ready{m}") for m in range(MH)]
        u_ready = [sem(f"u_ready{m}") for m in range(MH)]
        h1_psum = [sem(f"h1_psum{m}") for m in range(MH)]
        g1_ready = [sem(f"g1_ready{m}") for m in range(MH)]
        h2_psum = [sem(f"h2_psum{m}") for m in range(MH)]
        g2_ready = [sem(f"g2_ready{m}") for m in range(MH)]
        o_psum = sem("o_psum")
        on_ready = sem("on_ready")
        o_staged = sem("o_staged")
        out_stored = sem("out_stored")
        setup = sem("setup")

        N_WEIGHTS = 16
        STORES = 16 * (4 + TQ)
        block = ctx.enter_context(nc.Block())

        @block.sync
        def _(sync):
            for dst, src in ((ident[:, :], ident_in), (w_in[:, :], W_inT), (w_kqr[:, :], W_kqrT),
                             (w_v[:, :], W_vT), (w_beta[:, :], W_betaT), (bb[:, :], b_beta),
                             (w1[:, :], w1T), (w2[:, :], w2T),
                             (h1[:, :, :], h1T.rearrange("(m p) n -> p m n", p=P)),
                             (h2[:, :, :], h2T.rearrange("(m p) n -> p m n", p=P)),
                             (w3[:, :, :], w3T.rearrange("(m p) n -> p m n", p=P)),
                             (s1[:, :], w1_s), (s2[:, :], w2_s), (sh1[:, :], h1_s), (sh2[:, :], h2_s),
                             (s3[:, :], w3_s)):
                sync.dma_start(dst, src).then_inc(weights_in, 16)
            sync.wait_ge(w_out_zero, 1)
            for b in range(B):
                sync.dma_start(w_out[b * NB * IG:(b + 1) * NB * IG, :, b, :],
                               W_out_rows.rearrange("r (c d) -> r c d", c=NI)).then_inc(w_out_in, 16)
            with sync.Fori(0, B) as b:
                sync.wait_ge(xn_ready, b)
                sync.dma_start(x_in, x[bass.ds(b, 1)].rearrange("o (q p) d -> p (o q) d", p=P)
                               ).then_inc(x_loaded, 16)
                sync.wait_ge(v_staged, b + 1)
                sync.dma_start(v_d[bass.ds(b, 1)].rearrange("o p t -> (o p) t"), v_st).then_inc(stored, 16)
                sync.wait_ge(beta_staged, b + 1)
                sync.dma_start(beta_d[bass.ds(b, 1)].rearrange("o p t -> (o p) t"), beta_st).then_inc(stored, 16)
                sync.wait_ge(kq_staged, b * 2 + 2)
                sync.dma_start(q_d[bass.ds(b, 1)].rearrange("o (q p) j -> p (o q) j", p=P),
                               kq_st[:, :, NB * N:NB * N + N]).then_inc(stored, 16)
                sync.wait_ge(kn_staged, b + 1)
                for q in range(TQ):
                    sync.dma_start(kn_d[bass.ds(b, 1), :, q * P:(q + 1) * P, :].rearrange("o n p j -> p (o n) j"),
                                   kn_st[:, q]).then_inc(stored, 16)
                sync.wait_ge(r_staged, b + 1)
                sync.dma_start(r_d[bass.ds(b, 1)].rearrange("o r t -> (o r) t"), r_st[0:3 * NB, :]).then_inc(stored, 16)
            sync.wait_ge(stored, STORES * B)
            sync.dma_start(v_all[:, :, 0:T], v_d.rearrange("b (g i) t -> (b g) i t", i=NI)).then_inc(resident_in, 16)
            sync.dma_start(beta_all[:, :, 0:T], beta_d.rearrange("b (g i) t -> (b g) i t", i=NI)
                           ).then_inc(resident_in, 16)
            for k in range(3):
                for g in range(IG):
                    sync.dma_start(r_all[g:P:IG, k, 0:T], r_d[:, k * NB:(k + 1) * NB, :]).then_inc(resident_in, 16)

            def load_ring(t0, half):
                slots = slice(half * GR, (half + 1) * GR)
                for g in range(IG):
                    sync.dma_start(kn_ring[g:P:IG, slots].rearrange("p t j -> p (t j)"),
                                   kn_d[:, :, bass.ds(t0, GR), :].rearrange("b n t j -> (b n) (t j)")
                                   ).then_inc(ring_in[half], 16)
                for g in range(NB * IG):
                    sync.dma_start(q_ring[g:P:NB * IG, slots].rearrange("p t j -> p (t j)"),
                                   q_d[:, bass.ds(t0, GR), :].rearrange("b t j -> b (t j)")
                                   ).then_inc(ring_in[half], 16)

            def load_xt(c):
                for b in range(B):
                    sync.dma_start(xt[(b % 4) * CH:(b % 4 + 1) * CH, b // 4],
                                   x[b, bass.ds(c * CH, CH), :]).then_inc(xt_in, 16)

            def store_out(c):
                for b in range(B):
                    sync.dma_start(out[b, bass.ds(c * CH, CH), :],
                                   o_st[(b % 4) * CH:(b % 4 + 1) * CH, b // 4]).then_inc(out_stored, 16)

            def load_next(k):
                for half in range(2):
                    sync.wait_ge(q_used, k * CH + (half + 1) * GR + SR)
                    load_ring((k + 1) * CH + half * GR, half)

            for half in range(2):
                load_ring(half * GR, half)
            load_next(0)
            load_xt(0)
            load_next(1)
            with sync.Fori(2, NC - 1) as k:
                sync.wait_ge(x1_ready, k - 1)
                load_xt(k - 1)
                sync.wait_ge(o_staged, k - 1)
                store_out(k - 2)
                load_next(k)
            for k in (NC - 1, NC):
                sync.wait_ge(x1_ready, k - 1)
                load_xt(k - 1)
                sync.wait_ge(o_staged, k - 1)
                store_out(k - 2)
            sync.wait_ge(o_staged, NC)
            store_out(NC - 1)
            sync.wait_ge(out_stored, 16 * B * NC)

        RING_LOADS = 16 * (IG + NB * IG)
        RESIDENT = 16 * (2 + 3 * IG)
        HALF = [slice(h * HI, (h + 1) * HI) for h in range(2)]

        @block.gpsimd
        def _(pool):
            nc.gpsimd.memset(minus_half[:, :], -0.5)
            nc.gpsimd.memset(plus_half[:, :], 0.5).then_inc(consts_set, 1)
            pool.wait_ge(consts_set, 1)
            nc.gpsimd.memset(w_out[:, :, :, :].rearrange("p c b d -> p (c b d)"), 0.0).then_inc(w_out_zero, 1)
            for tile in (v_all, beta_all, r_all):
                nc.gpsimd.memset(tile[:, :, T:], 0.0).then_inc(padded, 1)
            with pool.Fori(0, B) as b:
                pool.wait_ge(var_ready, b + 1)
                nc.gpsimd.tensor_tensor(rstd, var_eps, minus_half[:, 0:TQ], ALU.pow).then_inc(rstd_ready, 1)
                pool.wait_ge(kq_staged, b * 2 + 2)
                nc.gpsimd.tensor_tensor(ksq, kq_st[:, :, 0:NB * N], kq_st[:, :, 0:NB * N], ALU.mult
                                        ).then_inc(ksq_ready, 1)
                pool.wait_ge(ss_ready, b + 1)
                nc.gpsimd.tensor_tensor(nrm, ss, plus_half[:, :], ALU.pow).then_inc(nrm_ready, 1)

            pool.wait_ge(resident_in, RESIDENT)
            pool.wait_ge(padded, 3)
            pool.wait_ge(state0, 1)

            def refill(t0, half):
                sl = slice(half * GR, (half + 1) * GR)
                nc.gpsimd.tensor_copy(Pk[:, sl, :, N].rearrange("p t i -> p i t"), v_all[:, :, bass.ds(t0, GR)])
                nc.gpsimd.tensor_copy(beta_ring[:, :, sl], beta_all[:, :, bass.ds(t0, GR)])
                nc.gpsimd.tensor_copy(w_ring[:, :, sl], r_all[:, 0:2, bass.ds(t0, GR)]).then_inc(filled[half], 1)

            def state_q(slot, v):
                pool.wait_ge(blended[1], v)
                nc.gpsimd.tensor_tensor(
                    Pq[slot // GR][:, :, slot % GR, :].rearrange("p j i -> p i j"), S[:, slot % SR],
                    q_ring[:, slot].unsqueeze(1).to_broadcast([P, NI, N]), ALU.mult).then_inc(q_used, 1)

            def pool_steps(k):
                for s in range(CH):
                    v = k * CH + (s + 1)
                    if s % GR == 0:
                        pool.wait_ge(filled[s // GR], k + 1)
                    for h in range(2):
                        pool.wait_ge(blended[h], v)
                        nc.gpsimd.tensor_tensor(bS[:, HALF[h]], S[:, (s - 1) % SR, HALF[h]],
                                                beta_ring[:, HALF[h], s].unsqueeze(2).to_broadcast([P, HI, N]),
                                                ALU.mult).then_inc(bS_ready[h], 1)
                    if s == 1:
                        if some(k):
                            pool.wait_ge(sq_psum[0], k)
                        pool.wait_ge(ring_in[0], (k + 1) * RING_LOADS)
                    if s == GR + 1:
                        if some(k):
                            pool.wait_ge(sq_psum[1], k)
                        pool.wait_ge(ring_in[1], (k + 1) * RING_LOADS)
                    if s or some(k):
                        state_q((s - 1) % CH, v)
                    if s == GR + 1:
                        refill(k * CH + CH, 0)
                    if s == 1:
                        if some(k):
                            refill(k * CH + GR, 1)
                    for at, n, c in ((16, 0, k), (21, 1, k), (25, 2, k - 1)):
                        if s == at and some(c):
                            inv_sqrt(n, c)

            def inv_sqrt(n, c):
                pool.wait_ge(cvar_ready[n], c)
                nc.gpsimd.tensor_tensor(crs[:, n], cve[:, n], minus_half[:, 0:BH], ALU.pow).then_inc(crs_ready[n], 1)

            for half in range(2):
                refill(half * GR, half)
            pool_steps(0)
            pool_steps(1)
            with pool.Fori(2, NC) as k:
                pool_steps(k)
            state_q(CH - 1, T + 1)
            inv_sqrt(2, NC - 1)
            inv_sqrt(0, NC)
            inv_sqrt(1, NC)
            inv_sqrt(2, NC)

        @block.scalar
        def _(act):
            act.wait_ge(weights_in, 16 * N_WEIGHTS)
            with act.Fori(0, B) as b:
                act.wait_ge(xnT_psum, b + 1)
                nc.scalar.activation(xnT, PS[:, 0, :], ACT.Copy).then_inc(xnT_ready, 1)
                act.wait_ge(xp_psum, b + 1)
                nc.scalar.activation(sg, PS[:, 1, :], ACT.Tanh, scale=0.5).then_inc(sg_ready, 1)
                act.wait_ge(v_psum, b + 1)
                act.wait_ge(stored, b * STORES)
                nc.scalar.activation(v_st, PS[:, 2, :], ACT.Copy, scale=-0.5).then_inc(v_staged, 1)
                act.wait_ge(beta_psum, b + 1)
                nc.scalar.activation(beta_th, PS[:, 3, :], ACT.Tanh, bias=bb_half[:, 0:1], scale=0.25
                                     ).then_inc(beta_tanh, 1)
                act.wait_ge(kq_psum, b + 1)
                for k in range(2):
                    nc.scalar.activation(kq_st[:, 2 * k:2 * k + 2, :],
                                         PS[:, 4 + k, 0:2 * KQ].rearrange("p (q c) -> p q c", q=2),
                                         ACT.Copy, scale=0.5).then_inc(kq_staged, 1)
                act.wait_ge(ld_ready, b + 1)
                nc.scalar.activation(lexp, ld, ACT.Exp).then_inc(lexp_ready, 1)
                act.wait_ge(r_psum, b + 1)
                nc.scalar.activation(r_st[0:3 * NB, :], PS[0:3 * NB, 6, :], ACT.Copy).then_inc(r_staged, 1)

            act.wait_ge(state0, 1)

            def keep(h, s, v):
                act.wait_ge(blended[h], v)
                nc.scalar.activation(G[:, HALF[h]], S[:, (s - 1) % SR, HALF[h]], ACT.Copy,
                                     scale=w_ring[:, 1, s:s + 1]).then_inc(G_ready[h], 1)

            def squash(h, v):
                act.wait_ge(pre_ready[h], v)
                nc.scalar.activation(U[:, HALF[h]], pre[:, HALF[h]], ACT.Tanh).then_inc(U_ready[h], 1)

            def sq_tanh_of(half, c):
                act.wait_ge(sq_psum[half], c)
                nc.scalar.activation(sq_th.rearrange("p t i -> p (t i)"), PS[:, half, 0:GR * NI], ACT.Tanh, scale=0.5
                                     ).then_inc(sq_tanh[half], 1)

            def copy_x1nT(c):
                act.wait_ge(x1nT_psum, c)
                nc.scalar.activation(x1nT, PS[:, 2, 0:TK], ACT.Copy).then_inc(x1nT_ready, 1)

            def save_x1(c):
                act.wait_ge(x1_ready, c)
                if some(c - 1):
                    act.wait_ge(o_staged, c - 1)
                nc.scalar.activation(x1_old, x1, ACT.Copy).then_inc(x1_saved, 1)

            def gate(m, c):
                act.wait_ge(gate_psum[m], c)
                nc.scalar.activation(gate_th[:, m % 2], PS[:, 4 + m % 2, 0:TK], ACT.Tanh,
                                     scale=s1_half[:, m:m + 1]).then_inc(gate_tanh[m], 1)

            def gelu(dst, psum, ready, scale, m, c):
                act.wait_ge(psum[m], c)
                nc.scalar.activation(dst[:, m], PS[:, 4 + m, 0:TK], ACT.Gelu, scale=scale[:, m:m + 1]
                                     ).then_inc(ready[m], 1)

            def act_between(s, k, c1, c2):
                if some(c2):
                    if 5 <= s < 5 + MH:
                        gelu(g1, h1_psum, g1_ready, sh1, s - 5, c2)
                    if s == 12:
                        save_x1(c2)
                    if 14 <= s < 14 + MH:
                        gelu(g2, h2_psum, g2_ready, sh2, s - 14, c2)
                if some(c1):
                    if s == 4:
                        sq_tanh_of(1, c1)
                    if s == 24:
                        copy_x1nT(c1)
                    if 26 <= s < 26 + MH:
                        gate(s - 26, c1)
                if s == 21:
                    sq_tanh_of(0, k + 1)

            def act_steps(k, c1, c2):
                for s in range(CH):
                    v = k * CH + (s + 1)
                    if s % GR == 0:
                        act.wait_ge(filled[s // GR], k + 1)
                    keep(0, s, v)
                    if s or some(k):
                        squash(1, v - 1)
                    squash(0, v)
                    keep(1, s, v)
                    act_between(s, k, c1, c2)

            act.wait_ge(scaled, 1)
            act_steps(0, 0, 0)
            act_steps(1, 1, 0)
            with act.Fori(2, NC) as k:
                act_steps(k, k, k - 1)
            squash(1, T)
            save_x1(NC - 1)
            for m in range(MH):
                gelu(g1, h1_psum, g1_ready, sh1, m, NC - 1)
            sq_tanh_of(1, NC)
            for m in range(MH):
                gelu(g2, h2_psum, g2_ready, sh2, m, NC - 1)
            save_x1(NC)
            copy_x1nT(NC)
            for m in range(MH):
                gate(m, NC)
            for m in range(MH):
                gelu(g1, h1_psum, g1_ready, sh1, m, NC)
            for m in range(MH):
                gelu(g2, h2_psum, g2_ready, sh2, m, NC)

        @block.vector
        def _(dve):
            dve.wait_ge(weights_in, 16 * N_WEIGHTS)
            sc = Count(dve, scaled, 1)
            nc.vector.tensor_scalar(s1_half[:, :], s1[:, :], 0.5, None, ALU.mult).then_inc(setup, 1)
            nc.vector.tensor_scalar(bb_half[:, :], bb[:, :], 0.5, None, ALU.mult)
            dve.wait_ge(setup, 1)
            nc.vector.tensor_tensor(s12[:, :], s1_half[:, :], s2[:, :], ALU.mult).then_inc(setup, 1)
            dve.wait_ge(setup, 2)
            for m in range(MH):
                nc.vector.tensor_scalar(h1[:, m], h1[:, m], s12[:, m:m + 1], None, ALU.mult)
                last = nc.vector.tensor_tensor(w3[:, m], w3[:, m], s3[:, :], ALU.mult)
            sc.inc(last)

            VA = 33
            with dve.Fori(0, B) as b:
                ch = Count(dve, va, VA)

                def link(ins):
                    ch.inc(ins)
                    ch.wait(b)

                dve.wait_ge(x_loaded, b * 16 + 16)
                for q in range(TQ):
                    ch.inc(nc.vector.bn_stats(stats[:, q], x_in[:, q]))
                ch.wait(b)
                nc.vector.memset(gate_v[:, :], 0.0)
                for q in range(TQ):
                    ch.inc(nc.vector.bn_aggr(mv[:, q], stats[:, q]))
                ch.wait(b)
                nc.vector.tensor_scalar(var_eps, mv[:, :, 1], EPS, None, ALU.add).then_inc(var_ready, 1)
                dve.wait_ge(rstd_ready, b + 1)
                dve.wait_ge(xnT_psum, b)
                for q in range(TQ):
                    last = nc.vector.tensor_scalar(xn[:, q], x_in[:, q], mv[:, q, 0:1], rstd[:, q:q + 1],
                                                   ALU.subtract, ALU.mult)
                last.then_inc(xn_ready, 1)
                dve.wait_ge(sg_ready, b + 1)
                nc.vector.scalar_tensor_tensor(out=xpT, in0=sg, scalar=1.0, in1=PS[:, 1, :], op0=ALU.add,
                                               op1=ALU.mult).then_inc(xp_ready, 1)
                dve.wait_ge(kq_staged, b * 2 + 2)
                lg = kq_st[:, :, NB * N + N:]
                link(nc.vector.tensor_reduce(lmax, lg, AX.X, ALU.max))
                nc.vector.tensor_tensor(ld, lg, lmax.unsqueeze(2).to_broadcast([P, TQ, NB]), ALU.subtract
                                        ).then_inc(ld_ready, 1)
                for n in range(NB):
                    link(nc.vector.memset(wins[:, :, n:n + 1], float(n)))
                for s in range(1, NB):
                    link(nc.vector.tensor_tensor(ge[:, :, 0:NB - s], lg[:, :, 0:NB - s], lg[:, :, s:NB], ALU.is_ge))
                    link(nc.vector.tensor_tensor(wins[:, :, 0:NB - s], wins[:, :, 0:NB - s], ge[:, :, 0:NB - s],
                                                 ALU.add))
                    link(nc.vector.tensor_tensor(wins[:, :, s:NB], wins[:, :, s:NB], ge[:, :, 0:NB - s],
                                                 ALU.subtract))
                link(nc.vector.tensor_scalar(mask, wins, float(NB - 2), None, ALU.is_ge))
                dve.wait_ge(lexp_ready, b + 1)
                link(nc.vector.tensor_reduce(lsum, lexp, AX.X, ALU.add))
                link(nc.vector.reciprocal(lsrec, lsum))
                dve.wait_ge(r_psum, b)
                link(nc.vector.tensor_tensor(r_tok[:, :, 2], lexp, lsrec.unsqueeze(2).to_broadcast([P, TQ, NB]),
                                             ALU.mult))
                link(nc.vector.tensor_tensor(uw, mask, r_tok[:, :, 2], ALU.mult))
                link(nc.vector.tensor_reduce(usum, uw, AX.X, ALU.add))
                link(nc.vector.tensor_scalar(usum_e, usum, 1e-8, None, ALU.add))
                link(nc.vector.reciprocal(urec, usum_e))
                link(nc.vector.tensor_tensor(r_tok[:, :, 0], uw, urec.unsqueeze(2).to_broadcast([P, TQ, NB]),
                                             ALU.mult))
                nc.vector.tensor_scalar(r_tok[:, :, 1], r_tok[:, :, 0], -1.0, 1.0, ALU.mult, ALU.add
                                        ).then_inc(r_tok_ready, 1)
                dve.wait_ge(stored, b * STORES)
                dve.wait_ge(beta_tanh, b + 1)
                nc.vector.tensor_scalar(beta_st, beta_th, 0.5, 0.5, ALU.mult, ALU.add).then_inc(beta_staged, 1)
                dve.wait_ge(ksq_ready, b + 1)
                nc.vector.tensor_reduce(ss, ksq.rearrange("p q (n j) -> p (q n) j", j=N), AX.X, ALU.add
                                        ).then_inc(ss_ready, 1)
                dve.wait_ge(nrm_ready, b + 1)
                link(nc.vector.tensor_scalar(nrm_eps, nrm, 1e-6, None, ALU.add))
                link(nc.vector.reciprocal(rnrm, nrm_eps))
                dve.wait_ge(stored, b * STORES)
                for q in range(TQ):
                    last = nc.vector.tensor_tensor(
                        kn_st[:, q], kq_st[:, q, 0:NB * N].rearrange("p (n j) -> p n j", j=N),
                        rnrm[:, q * NB:(q + 1) * NB].unsqueeze(2).to_broadcast([P, NB, N]), ALU.mult)
                last.then_inc(kn_staged, 1)
                ch.close()

            dve.wait_ge(stored, STORES * B)
            nc.vector.memset(gate_v[:, :], 0.0).then_inc(state0, 1)
            for h in range(2):
                nc.vector.memset(S[:, :, HALF[h]], 0.0).then_inc(blended[h], 1)
            nc.vector.memset(outer, 0.0).then_inc(q_used, SR)

            def product(h, s, v):
                dve.wait_ge(blended[h], v)
                nc.vector.tensor_tensor(Pk[:, s, HALF[h], 0:N], S[:, (s - 1) % SR, HALF[h]],
                                        kn_ring[:, s].unsqueeze(1).to_broadcast([P, HI, N]), ALU.mult
                                        ).then_inc(Pk_ready[h], 1)

            def retrieve(h, s, v):
                dve.wait_ge(Pk_ready[h], v)
                nc.vector.tensor_reduce(delta[:, HALF[h]], Pk[:, s, HALF[h]], AX.X, ALU.add, negate=True
                                        ).then_inc(delta_ready[h], 1)

            def outer_product(h, s, v):
                dve.wait_ge(delta_ready[h], v)
                nc.vector.tensor_tensor(outer[:, HALF[h]], delta[:, HALF[h]].unsqueeze(2).to_broadcast([P, HI, N]),
                                        kn_ring[:, s].unsqueeze(1).to_broadcast([P, HI, N]), ALU.mult
                                        ).then_inc(outer_ready[h], 1)

            def add_decayed(h, v):
                dve.wait_ge(outer_ready[h], v)
                dve.wait_ge(bS_ready[h], v)
                nc.vector.tensor_tensor(pre[:, HALF[h]], outer[:, HALF[h]], bS[:, HALF[h]], ALU.add
                                        ).then_inc(pre_ready[h], 1)

            def blend(h, s, v):
                dve.wait_ge(U_ready[h], v)
                dve.wait_ge(G_ready[h], v)
                if h == 0:
                    dve.wait_ge(q_used, v)
                nc.vector.scalar_tensor_tensor(out=S[:, s % SR, HALF[h]], in0=U[:, HALF[h]],
                                               scalar=w_ring[:, 0, s:s + 1], in1=G[:, HALF[h]],
                                               op0=ALU.mult, op1=ALU.add).then_inc(blended[h], 1)

            def readout(n, half, c):
                pv = PS[:, half, 0:GR * NI].rearrange("p (t i) -> p t i", i=NI)
                if n == 0:
                    dve.wait_ge(sq_tanh[half], c)
                    nc.vector.scalar_tensor_tensor(out=sq_a, in0=sq_th, scalar=1.0, in1=pv, op0=ALU.add, op1=ALU.mult
                                                   ).then_inc(sq_a_ready[half], 1)
                if n == 1:
                    dve.wait_ge(sq_a_ready[half], c)
                    nc.vector.scalar_tensor_tensor(out=sq_b, in0=sq_a, scalar=0.5, in1=pv, op0=ALU.mult, op1=ALU.mult
                                                   ).then_inc(sq_b_ready[half], 1)
                if n == 2:
                    dve.wait_ge(sq_b_ready[half], c)
                    nc.vector.tensor_tensor(bo[:, :, half * GR:(half + 1) * GR].rearrange("p i t -> p t i"), sq_b,
                                            r_all[:, 2, bass.ds(c * CH - CH + half * GR, GR)].unsqueeze(2)
                                            .to_broadcast([P, GR, NI]), ALU.mult).then_inc(bo_ready[half], 1)

            def norm_stats(n, src, bh, ready, c):
                if bh == 0:
                    dve.wait_ge(ready, c)
                ins = nc.vector.bn_stats(cst[:, n, bh], src[:, bh])
                if bh == BH - 1:
                    ins.then_inc(stats_ready[n], 1)

            def norm_aggr(n, c):
                dve.wait_ge(stats_ready[n], c)
                nc.vector.memset(gate_v[:, :], 0.0)
                for bh in range(BH):
                    last = nc.vector.bn_aggr(cmv[:, n, bh], cst[:, n, bh])
                last.then_inc(aggr_ready[n], 1)

            def norm_var(n, c):
                dve.wait_ge(aggr_ready[n], c)
                nc.vector.tensor_scalar(cve[:, n], cmv[:, n, :, 1], EPS, None, ALU.add).then_inc(cvar_ready[n], 1)

            def norm_apply(n, dst, src, bh, ready, c):
                dve.wait_ge(crs_ready[n], c)
                ins = nc.vector.tensor_scalar(dst[:, bh], src[:, bh], cmv[:, n, bh, 0:1], crs[:, n, bh:bh + 1],
                                              ALU.subtract, ALU.mult)
                if bh == BH - 1:
                    ins.then_inc(ready, 1)

            psY = PS[:, 2, 0:BH * D].rearrange("p (b d) -> p b d", d=D)
            psO = PS[:, 3, 0:BH * D].rearrange("p (b d) -> p b d", d=D)

            def residual(c):
                dve.wait_ge(yn_ready, c)
                dve.wait_ge(xt_in, c * (16 * B))
                if some(c - 1):
                    dve.wait_ge(x1_saved, c - 1)
                nc.vector.tensor_tensor(x1, xt, yn, ALU.add).then_inc(x1_ready, 1)

            def result(c):
                dve.wait_ge(on_ready, c)
                if some(c - 1):
                    dve.wait_ge(out_stored, (c - 1) * (16 * B))
                dve.wait_ge(x1_saved, c)
                nc.vector.tensor_tensor(o_st, x1_old, on, ALU.add).then_inc(o_staged, 1)

            def gate_product(m, c):
                dve.wait_ge(gate_tanh[m], c)
                nc.vector.scalar_tensor_tensor(out=gate_t[:, m % 2], in0=gate_th[:, m % 2], scalar=1.0,
                                               in1=PS[:, 4 + m % 2, 0:TK], op0=ALU.add, op1=ALU.mult
                                               ).then_inc(gate_ready[m], 1)

            def up_product(m, c):
                dve.wait_ge(gate_ready[m], c)
                nc.vector.tensor_tensor(u[:, m], gate_t[:, m % 2], PS[:, 6 + m % 2, 0:TK], ALU.mult
                                        ).then_inc(u_ready[m], 1)

            def dve_between(s, slot, k, c1, c2):
                at = (s, slot)
                if some(c1):
                    if at in ((5, 1), (6, 0), (6, 1)):
                        readout((s * 2 + slot) - 11, 1, c1)
                    if at in ((14, 0), (14, 1)):
                        norm_stats(0, psY, slot, y_psum, c1)
                    if at == (15, 0):
                        norm_aggr(0, c1)
                    if at == (15, 1):
                        norm_var(0, c1)
                    if at in ((17, 0), (17, 1)):
                        norm_apply(0, yn, psY, slot, yn_ready, c1)
                    if at == (18, 0):
                        residual(c1)
                    if at in ((18, 1), (19, 0)):
                        norm_stats(1, x1, 1 - slot, x1_ready, c1)
                    if at == (19, 1):
                        norm_aggr(1, c1)
                    if at == (20, 0):
                        norm_var(1, c1)
                    if at in ((22, 0), (22, 1)):
                        norm_apply(1, x1n, x1, slot, x1n_ready, c1)
                    if 27 <= s < 27 + MH:
                        if slot == 0:
                            gate_product(s - 27, c1)
                        else:
                            up_product(s - 27, c1)
                if some(c2):
                    if at in ((21, 0), (21, 1)):
                        norm_stats(2, psO, slot, o_psum, c2)
                    if at == (23, 0):
                        norm_aggr(2, c2)
                    if at == (23, 1):
                        norm_var(2, c2)
                    if at in ((26, 0), (26, 1)):
                        norm_apply(2, on, psO, slot, on_ready, c2)
                    if at == (31, 0):
                        result(c2)
                if at in ((24, 0), (24, 1), (25, 0)):
                    readout((s * 2 + slot) - 48, 0, k + 1)

            def dve_steps(k, c1, c2):
                for s in range(CH):
                    first = not some(k) and s == 0
                    v = k * CH + (s + 1)
                    before = (s - 1) % CH
                    if s % GR == 0:
                        dve.wait_ge(filled[s // GR], k + 1)
                        dve.wait_ge(ring_in[s // GR], (k + 1) * RING_LOADS)
                    product(0, s, v)
                    if not first:
                        outer_product(1, before, v - 1)
                    retrieve(0, s, v)
                    if not first:
                        add_decayed(1, v - 1)
                    outer_product(0, s, v)
                    dve_between(s, 0, k, c1, c2)
                    add_decayed(0, v)
                    if not first:
                        blend(1, before, v - 1)
                    dve_between(s, 1, k, c1, c2)
                    product(1, s, v)
                    blend(0, s, v)
                    retrieve(1, s, v)

            dve_steps(0, 0, 0)
            dve_steps(1, 1, 0)
            with dve.Fori(2, NC) as k:
                dve_steps(k, k, k - 1)
            outer_product(1, CH - 1, T)
            add_decayed(1, T)
            blend(1, CH - 1, T)
            for n in range(3):
                readout(n, 1, NC)

            def last_norm(c):
                for bh in range(BH):
                    norm_stats(2, psO, bh, o_psum, c)
                norm_aggr(2, c)
                norm_var(2, c)
                for bh in range(BH):
                    norm_apply(2, on, psO, bh, on_ready, c)
                result(c)

            last_norm(NC - 1)
            for bh in range(BH):
                norm_stats(0, psY, bh, y_psum, NC)
            norm_aggr(0, NC)
            norm_var(0, NC)
            for bh in range(BH):
                norm_apply(0, yn, psY, bh, yn_ready, NC)
            residual(NC)
            for bh in range(BH):
                norm_stats(1, x1, bh, x1_ready, NC)
            norm_aggr(1, NC)
            norm_var(1, NC)
            for bh in range(BH):
                norm_apply(1, x1n, x1, bh, x1n_ready, NC)
            for m in range(MH):
                gate_product(m, NC)
                up_product(m, NC)
            last_norm(NC)

        @block.tensor
        def _(pe):
            pe.wait_ge(weights_in, 16 * N_WEIGHTS)
            with pe.Fori(0, B) as b:
                pe.wait_ge(xn_ready, b + 1)
                for q in range(TQ):
                    last = nc.tensor.transpose(PS[:, 0, q * P:(q + 1) * P], xn[:, q], ident[:, :])
                last.then_inc(xnT_psum, 1)
                pe.wait_ge(xnT_ready, b + 1)
                nc.tensor.matmul(PS[:, 1, :], w_in[:, :], xnT, start=True, stop=True).then_inc(xp_psum, 1)
                pe.wait_ge(xp_ready, b + 1)
                nc.tensor.matmul(PS[:, 2, :], w_v[:, :], xpT, start=True, stop=True).then_inc(v_psum, 1)
                nc.tensor.matmul(PS[:, 3, :], w_beta[:, :], xpT, start=True, stop=True).then_inc(beta_psum, 1)
                for q in range(TQ):
                    last = nc.tensor.matmul(PS[:, 4 + q // 2, (q % 2) * KQ:(q % 2 + 1) * KQ],
                                            xpT[:, q * P:(q + 1) * P], w_kqr[:, :], start=(q % 2 == 0), stop=True,
                                            skip_group_check=True)
                last.then_inc(kq_psum, 1)
                pe.wait_ge(r_tok_ready, b + 1)
                for q in range(TQ):
                    last = nc.tensor.transpose(PS[0:3 * NB, 6, q * P:(q + 1) * P],
                                               r_tok[:, q].rearrange("p k n -> p (k n)"), ident[:, :])
                last.then_inc(r_psum, 1)

            pe.wait_ge(w_out_in, 16 * B)
            pe.wait_ge(scaled, 1)

            def sum_q(half, k):
                pe.wait_ge(q_used, k * CH + (half + 1) * GR + SR)
                if some(k):
                    pe.wait_ge(bo_ready[half], k)
                for j in range(N):
                    last = nc.tensor.matmul(PS[:, half, 0:GR * NI], ident[:, :],
                                            Pq[half][:, j].rearrange("p t i -> p (t i)"),
                                            start=(j == 0), stop=(j == N - 1))
                last.then_inc(sq_psum[half], 1)

            def project(c):
                for half in range(2):
                    pe.wait_ge(bo_ready[half], c)
                for b in range(B):
                    for i in range(NI):
                        last = nc.tensor.matmul(PS[(b % 4) * CH:(b % 4 + 1) * CH, 2, (b // 4) * D:(b // 4 + 1) * D],
                                                bo[:, i], w_out[:, i, b],
                                                start=(i == 0), stop=(i == NI - 1), skip_group_check=True)
                last.then_inc(y_psum, 1)

            def transpose_x1n(c):
                pe.wait_ge(x1n_ready, c)
                for bh in range(BH):
                    last = nc.tensor.transpose(PS[:, 2, bh * P:(bh + 1) * P], x1n[:, bh], ident[:, :])
                last.then_inc(x1nT_psum, 1)

            def gate_up(c):
                pe.wait_ge(x1nT_ready, c)
                for m in range(MH):
                    if m >= 2:
                        pe.wait_ge(u_ready[m - 2], c)
                    nc.tensor.matmul(PS[:, 6 + m % 2, 0:TK], w2[:, m * P:(m + 1) * P], x1nT, start=True, stop=True)
                    nc.tensor.matmul(PS[:, 4 + m % 2, 0:TK], w1[:, m * P:(m + 1) * P], x1nT, start=True, stop=True
                                     ).then_inc(gate_psum[m], 1)

            def hidden(w, src, src_ready, psum, c):
                for k in range(MH):
                    pe.wait_ge(src_ready[k], c)
                for m in range(MH):
                    for k in range(MH):
                        last = nc.tensor.matmul(PS[:, 4 + m, 0:TK], w[:, k, m * P:(m + 1) * P], src[:, k],
                                                start=(k == 0), stop=(k == MH - 1))
                    last.then_inc(psum[m], 1)

            def down(c):
                for k in range(MH):
                    pe.wait_ge(g2_ready[k], c)
                for bh in range(BH):
                    for k in range(MH):
                        last = nc.tensor.matmul(PS[:, 3, bh * D:(bh + 1) * D], g2[:, k, bh * P:(bh + 1) * P], w3[:, k],
                                                start=(k == 0), stop=(k == MH - 1), skip_group_check=True)
                last.then_inc(o_psum, 1)

            def pe_turn(k, c1, c2):
                if some(c1):
                    sum_q(1, k - 1)
                if some(c2):
                    hidden(h1, u, u_ready, h1_psum, c2)
                if some(c1):
                    project(c1)
                if some(c2):
                    hidden(h2, g1, g1_ready, h2_psum, c2)
                sum_q(0, k)
                if some(c2):
                    down(c2)
                if some(c1):
                    transpose_x1n(c1)
                    gate_up(c1)

            pe_turn(0, 0, 0)
            pe_turn(1, 1, 0)
            with pe.Fori(2, NC) as k:
                pe_turn(k, k, k - 1)
            sum_q(1, NC - 1)
            hidden(h1, u, u_ready, h1_psum, NC - 1)
            hidden(h2, g1, g1_ready, h2_psum, NC - 1)
            down(NC - 1)
            project(NC)
            transpose_x1n(NC)
            gate_up(NC)
            hidden(h1, u, u_ready, h1_psum, NC)
            hidden(h2, g1, g1_ready, h2_psum, NC)
            down(NC)


def kernel(L0_attn_x, L0_attn_W_in, L0_attn_W_router, L0_attn_W_kv, L0_attn_W_beta, L0_attn_b_beta,
           L0_attn_W_q, L0_attn_W_out, L0_ffn_w1_w, L0_ffn_w1_s, L0_ffn_w2_w, L0_ffn_w2_s, L0_ffn_h1_w,
           L0_ffn_h1_s, L0_ffn_h2_w, L0_ffn_h2_s, L0_ffn_w3_w, L0_ffn_w3_s):
    import numpy as np
    import concourse.bacc as bacc
    from concourse.bass_utils import run_bass_kernel_spmd

    D = L0_attn_x.shape[2]
    NB, N = L0_attn_b_beta.shape
    IG = 4
    kv = np.asarray(L0_attn_W_kv).reshape(NB, 2, N, D)
    W_k = kv[:, 0].reshape(NB * N, D)
    W_v = kv[:, 1].reshape(NB * N, D)

    def column(s):
        return np.asarray(s).reshape(-1, 128).T

    W_out_rows = np.asarray(L0_attn_W_out).T.reshape(IG, (N // IG) * D)
    arrays = {
        "x": L0_attn_x,
        "W_inT": np.asarray(L0_attn_W_in).T,
        "W_kqrT": np.concatenate([W_k, np.asarray(L0_attn_W_q), np.asarray(L0_attn_W_router)]).T,
        "W_vT": W_v.T,
        "W_betaT": np.asarray(L0_attn_W_beta).T,
        "b_beta": np.asarray(L0_attn_b_beta).reshape(NB * N, 1),
        "W_out_rows": np.tile(W_out_rows, (NB, 1)),
        "w1T": np.asarray(L0_ffn_w1_w).T,
        "w2T": np.asarray(L0_ffn_w2_w).T,
        "h1T": np.asarray(L0_ffn_h1_w).T,
        "h2T": np.asarray(L0_ffn_h2_w).T,
        "w3T": np.asarray(L0_ffn_w3_w).T,
        "w1_s": column(L0_ffn_w1_s),
        "w2_s": column(L0_ffn_w2_s),
        "h1_s": column(L0_ffn_h1_s),
        "h2_s": column(L0_ffn_h2_s),
        "w3_s": np.tile(np.asarray(L0_ffn_w3_s), (128, 1)),
        "ident_in": np.eye(128, dtype=np.float32),
    }
    nc = bacc.Bacc("TRN2", target_bir_lowering=False, num_devices=1)
    feeds, args = {}, []
    for name, a in arrays.items():
        a = np.ascontiguousarray(a)
        feeds[name + "_dram"] = a
        args.append(nc.dram_tensor(name + "_dram", a.shape, mybir.dt.from_np(a.dtype), kind="ExternalInput").ap())
    args.append(nc.dram_tensor("out_dram", np.asarray(L0_attn_x).shape, F32, kind="ExternalOutput").ap())
    sandwich(nc, *args)
    r = run_bass_kernel_spmd(nc, [feeds], core_ids=[0])
    return r.results[0]["out_dram"]
```

```python
import concourse.bass as bass
from concourse import mybir
from contextlib import ExitStack


F32 = mybir.dt.float32
ALU = mybir.AluOpType
ACT = mybir.ActivationFunctionType
AX = mybir.AxisListType




def some(count):
    return not isinstance(count, int) or count > 0


def sandwich(nc, x, W_inT, W_kqrT, W_vT, W_betaT, b_beta, W_out_rows, w1T, w2T, h1T, h2T, w3T,
             w1_s, w2_s, h1_s, h2_s, w3_s, ident_in, own_seq_in, out):
    B, T, D = x.shape
    P = 128
    NB = 4
    N = 32
    IG = P // (B * NB)
    NI = N // IG
    HI = NI // 2
    TQ = T // P
    KQ = NB * N + N + NB
    CH = 32
    GR = CH // 2
    NC = T // CH
    BH = B // 4
    SR = 4
    HID = w1T.shape[1]
    MH = HID // P
    EPS = 1e-5

    with ExitStack() as ctx:
        def sb(name, shape):
            return ctx.enter_context(nc.sbuf_tensor(name, shape, F32))

        def sem(name):
            return ctx.enter_context(nc.semaphore(name))

        kn_d = nc.dram_tensor("kn_scratch", (B, NB, T, N), F32, kind="Internal").ap()
        q_d = nc.dram_tensor("q_scratch", (B, T, N), F32, kind="Internal").ap()

        ident = sb("ident", [P, P])
        w_in = sb("w_in", [P, P])
        w_kqr = sb("w_kqr", [P, KQ])
        w_v = sb("w_v", [P, P])
        w_beta = sb("w_beta", [P, P])
        bb = sb("bb", [P, 1])
        w1 = sb("w1", [P, HID])
        w2 = sb("w2", [P, HID])
        h1 = sb("h1", [P, MH, HID])
        h2 = sb("h2", [P, MH, HID])
        w3 = sb("w3", [P, MH, D])
        s1 = sb("s1", [P, MH])
        s2 = sb("s2", [P, MH])
        sh1 = sb("sh1", [P, MH])
        sh2 = sb("sh2", [P, MH])
        s3 = sb("s3", [P, D])
        s12 = sb("s12", [P, MH])
        s1_half = sb("s1_half", [P, MH])
        bb_half = sb("bb_half", [P, 1])
        spacer = sb("spacer", [P, 1])
        warm = sb("warm", [P, 1])
        minus_half = sb("minus_half", [P, 16])

        v_all = sb("v_all", [P, NI, T + GR])
        beta_all = sb("beta_all", [P, NI, T + GR])
        r_all = sb("r_all", [P, 3, T + GR])
        w_out = sb("w_out", [P, NI, D])
        own_seq = sb("own_seq", [P, B])

        REG = 30600
        region = sb("region", [P, REG])
        taken = [0]

        def carve(*shape):
            n = 1
            for s in shape:
                n *= s
            a = region[:, taken[0]:taken[0] + n]
            taken[0] += n
            assert taken[0] <= REG
            if len(shape) == 1:
                return a
            names = "abcd"[:len(shape)]
            return a.rearrange(f"p ({' '.join(names)}) -> p {' '.join(names)}", **dict(zip(names, shape)))

        QB = TQ * B
        x_in = carve(2, TQ, D)
        xn = carve(2, TQ, D)
        xnT = carve(T)
        sg = carve(T)
        xpT = carve(2, T)
        v_st = carve(2, T)
        beta_th = carve(2, T)
        beta_st = carve(2, T)
        ln_stat = carve(TQ, 6)
        mv = carve(2, TQ, 2)
        var_eps = carve(TQ)
        rstd = carve(TQ)
        ss = carve(QB * NB)
        nrm = carve(QB * NB)
        nrm_eps = carve(QB * NB)
        rnrm = carve(QB * NB)
        lmax = carve(QB)
        ld = carve(QB, NB)
        lexp = carve(QB, NB)
        lsum = carve(QB)
        lsrec = carve(QB)
        ge = carve(QB, NB)
        wins = carve(QB, NB)
        mask = carve(QB, NB)
        uw = carve(QB, NB)
        usum = carve(QB)
        usum_e = carve(QB)
        urec = carve(QB)
        soft = carve(QB, NB)
        r_tok = carve(3, QB * NB, IG)
        taken[0] = REG - QB * (KQ + NB * N)
        kq_st = carve(QB, KQ)
        kn_st = carve(QB, NB, N)
        taken[0] = 0
        kn_ring = carve(CH, N)
        q_ring = carve(CH, N)
        beta_ring = carve(NI, CH)
        w_ring = carve(2, CH)
        sm_ring = carve(CH)
        S = carve(SR, NI, N)
        Pk = carve(CH, NI, N + 1)
        delta = carve(NI)
        outer = carve(NI, N)
        bS = carve(NI, N)
        pre = carve(NI, N)
        U = carve(NI, N)
        G = carve(NI, N)
        Pq = [carve(N, GR, NI) for _ in range(2)]
        sq_th = carve(GR, NI)
        sq_a = carve(GR, NI)
        sq_b = carve(GR, NI)
        bo = carve(NI, CH)
        bo_own = carve(NI, B, CH)
        TK = B * CH
        xt = carve(BH, D)
        yn = carve(BH, D)
        x1 = carve(BH, D)
        x1_old = carve(BH, D)
        x1n = carve(BH, D)
        x1nT = carve(TK)
        gate_th = carve(2, TK)
        gate_t = carve(2, TK)
        up = carve(2, TK)
        u = carve(MH, TK)
        g1 = carve(MH, TK)
        g2 = u
        on = carve(BH, D)
        o_st = carve(BH, D)
        cst = carve(3, BH, 6)
        cmv = carve(3, BH, 2)
        cve = carve(3, BH)
        crs = carve(3, BH)
        minus_mean = carve(3, BH)
        shift = carve(3, BH)

        PS = ctx.enter_context(nc.psum_tensor("PS", [P, 8, 512], F32))

        weights_in = sem("weights_in")
        consts_set = sem("consts_set")
        bb_ready = sem("bb_ready")
        scaled = sem("scaled")
        ffn_weights_in = sem("ffn_weights_in")
        x_loaded = [sem(f"x_loaded{p}") for p in range(2)]
        ln_stats = sem("ln_stats")
        ln_aggr = sem("ln_aggr")
        var_ready = sem("var_ready")
        rstd_ready = sem("rstd_ready")
        xn_ready = sem("xn_ready")
        xnT_psum = sem("xnT_psum")
        xnT_ready = sem("xnT_ready")
        xp_psum = sem("xp_psum")
        sg_ready = sem("sg_ready")
        xp_ready = sem("xp_ready")
        v_psum = sem("v_psum")
        beta_psum = sem("beta_psum")
        kq_psum = sem("kq_psum")
        v_staged = sem("v_staged")
        beta_tanh = sem("beta_tanh")
        beta_staged = sem("beta_staged")
        kq_staged = sem("kq_staged")
        v_stored = [sem(f"v_stored{p}") for p in range(2)]
        beta_stored = [sem(f"beta_stored{p}") for p in range(2)]
        ksq_ready = sem("ksq_ready")
        ss_ready = sem("ss_ready")
        nrm_ready = sem("nrm_ready")
        kn_staged = sem("kn_staged")
        kq_stored = sem("kq_stored")
        ld_ready = sem("ld_ready")
        lexp_ready = sem("lexp_ready")
        router = sem("router")
        soft_ready = sem("soft_ready")
        soft_spread = sem("soft_spread")
        r_tok_ready = sem("r_tok_ready")
        r_psum = sem("r_psum")
        r_ready = sem("r_ready")

        padded = sem("padded")
        ring_in = [sem(f"ring_in{h}") for h in range(2)]
        filled = [sem(f"filled{h}") for h in range(2)]
        state0 = sem("state0")
        blended = [sem(f"blended{h}") for h in range(2)]
        Pk_ready = [sem(f"Pk_ready{h}") for h in range(2)]
        delta_ready = [sem(f"delta_ready{h}") for h in range(2)]
        outer_ready = [sem(f"outer_ready{h}") for h in range(2)]
        bS_ready = [sem(f"bS_ready{h}") for h in range(2)]
        pre_ready = [sem(f"pre_ready{h}") for h in range(2)]
        U_ready = [sem(f"U_ready{h}") for h in range(2)]
        G_ready = [sem(f"G_ready{h}") for h in range(2)]
        q_used = sem("q_used")
        sq_psum = [sem(f"sq_psum{h}") for h in range(2)]
        sq_a_ready = [sem(f"sq_a_ready{h}") for h in range(2)]
        sq_b_ready = [sem(f"sq_b_ready{h}") for h in range(2)]
        bo_ready = [sem(f"bo_ready{h}") for h in range(2)]
        sm_ready = sem("sm_ready")
        bo_spread = sem("bo_spread")
        xt_in = sem("xt_in")
        y_psum = sem("y_psum")
        stats_ready = [sem(f"stats_ready{k}") for k in range(3)]
        aggr_ready = [sem(f"aggr_ready{k}") for k in range(3)]
        cvar_ready = [sem(f"cvar_ready{k}") for k in range(3)]
        crs_ready = [sem(f"crs_ready{k}") for k in range(3)]
        scale_ready = [sem(f"scale_ready{k}") for k in range(3)]
        yn_ready = sem("yn_ready")
        x1_ready = sem("x1_ready")
        x1_saved = sem("x1_saved")
        x1n_ready = sem("x1n_ready")
        x1nT_psum = sem("x1nT_psum")
        x1nT_ready = sem("x1nT_ready")
        gate_psum = [sem(f"gate_psum{m}") for m in range(MH)]
        gate_tanh = [sem(f"gate_tanh{m}") for m in range(MH)]
        up_ready = [sem(f"up_ready{m}") for m in range(MH)]
        gate_ready = [sem(f"gate_ready{m}") for m in range(MH)]
        u_ready = [sem(f"u_ready{m}") for m in range(MH)]
        h1_psum = [sem(f"h1_psum{m}") for m in range(MH)]
        g1_ready = [sem(f"g1_ready{m}") for m in range(MH)]
        h2_psum = [sem(f"h2_psum{m}") for m in range(MH)]
        g2_ready = [sem(f"g2_ready{m}") for m in range(MH)]
        o_psum = sem("o_psum")
        on_ready = sem("on_ready")
        o_staged = sem("o_staged")
        out_stored = sem("out_stored")
        setup = sem("setup")

        PROJ_WEIGHTS = 16 * 6
        FFN_WEIGHTS = 16 * 12
        CHUNK_DMAS = 16 * BH
        PAIRS = B // 2
        block = ctx.enter_context(nc.Block())

        @block.sync
        def _(sync):
            def load_x(b, p):
                sync.dma_start(x_in[:, p], x[bass.ds(b, 1)].rearrange("o (q p) d -> p (o q) d", p=P)
                               ).then_inc(x_loaded[p], 16)

            def spread(b, p):
                own = bass.ds(b * NB * IG, NB * IG)
                sync.wait_ge(v_staged, b + 1)
                sync.dma_start(v_all[own, :, 0:T], v_st[:, p]).then_inc(v_stored[p], 16)
                sync.wait_ge(beta_staged, b + 1)
                sync.dma_start(beta_all[own, :, 0:T], beta_st[:, p]).then_inc(beta_stored[p], 16)

            load_x(0, 0)
            for dst, src in ((ident[:, :], ident_in), (w_in[:, :], W_inT)):
                sync.dma_start(dst, src).then_inc(weights_in, 16)
            load_x(1, 1)
            for dst, src in ((w_v[:, :], W_vT), (w_kqr[:, :], W_kqrT), (w_beta[:, :], W_betaT),
                             (bb[:, :], b_beta)):
                sync.dma_start(dst, src).then_inc(weights_in, 16)
            for p in range(2):
                sync.wait_ge(xn_ready, p + 1)
                load_x(2 + p, p)
            for b in range(B):
                if b < B - 4:
                    sync.wait_ge(xn_ready, b + 3)
                    load_x(b + 4, b % 2)
                if b == B - 4:
                    for dst, src in ((w1[:, :], w1T), (w2[:, :], w2T),
                                     (h1[:, :, :], h1T.rearrange("(m p) n -> p m n", p=P)),
                                     (h2[:, :, :], h2T.rearrange("(m p) n -> p m n", p=P)),
                                     (w3[:, :, :], w3T.rearrange("(m p) n -> p m n", p=P)),
                                     (s1[:, :], w1_s), (s2[:, :], w2_s), (sh1[:, :], h1_s), (sh2[:, :], h2_s),
                                     (s3[:, :], w3_s), (own_seq[:, :], own_seq_in),
                                     (w_out[:, :, :], W_out_rows.rearrange("r (c d) -> r c d", c=NI))):
                        sync.dma_start(dst, src).then_inc(ffn_weights_in, 16)
                spread(b, b % 2)

            def store_kq(q):
                tiles = slice(q * B, (q + 1) * B)
                sync.wait_ge(kn_staged, q + 1)
                sync.dma_start(kn_d[:, :, q * P:(q + 1) * P, :].rearrange("b n p j -> p (b n) j"),
                               kn_st[:, tiles].rearrange("p b n j -> p (b n) j")).then_inc(kq_stored, 16)
                sync.dma_start(q_d[:, q * P:(q + 1) * P, :].rearrange("b p j -> p b j"),
                               kq_st[:, tiles, NB * N:NB * N + N]).then_inc(kq_stored, 16)

            def load_ring(t0, half):
                slots = slice(half * GR, (half + 1) * GR)
                sync.dma_start(kn_ring[:, slots].rearrange("p t j -> p (t j)"),
                               kn_d[:, :, bass.ds(t0, GR), :].rearrange("b n t j -> (b n) (t j)")
                               .unsqueeze(1).to_broadcast([B * NB, IG, GR * N])).then_inc(ring_in[half], 16)
                sync.dma_start(q_ring[:, slots].rearrange("p t j -> p (t j)"),
                               q_d[:, bass.ds(t0, GR), :].rearrange("b t j -> b (t j)")
                               .unsqueeze(1).to_broadcast([B, NB * IG, GR * N])).then_inc(ring_in[half], 16)

            def load_xt(c):
                for bh in range(BH):
                    sync.dma_start(xt[:, bh], x[4 * bh:4 * bh + 4, bass.ds(c * CH, CH), :]).then_inc(xt_in, 16)

            def store_out(c):
                for bh in range(BH):
                    sync.dma_start(out[4 * bh:4 * bh + 4, bass.ds(c * CH, CH), :], o_st[:, bh]
                                   ).then_inc(out_stored, 16)

            def load_next(k, half):
                sync.wait_ge(q_used, k * CH + (half + 1) * GR + SR)
                load_ring((k + 1) * CH + half * GR, half)

            store_kq(0)
            sync.wait_ge(kq_stored, 2 * 16)
            for half in range(2):
                load_ring(half * GR, half)
            for q in range(1, TQ):
                store_kq(q)
            sync.wait_ge(kq_stored, 2 * 16 * TQ)
            for half in range(2):
                load_next(0, half)
            load_xt(0)
            for half in range(2):
                load_next(1, half)
            with sync.Fori(2, NC - 1) as k:
                sync.wait_ge(x1_ready, k - 1)
                load_xt(k - 1)
                load_next(k, 0)
                sync.wait_ge(o_staged, k - 1)
                store_out(k - 2)
                load_next(k, 1)
            for k in (NC - 1, NC):
                sync.wait_ge(x1_ready, k - 1)
                load_xt(k - 1)
                sync.wait_ge(o_staged, k - 1)
                store_out(k - 2)
            sync.wait_ge(o_staged, NC)
            store_out(NC - 1)
            sync.wait_ge(out_stored, CHUNK_DMAS * NC)

        RING_LOADS = 16 * 2
        GATE_STEPS = (25, 26, 28, 29)
        psY = PS[:, 2, 0:BH * D].rearrange("p (b d) -> p b d", d=D)
        psO = PS[:, 3, 0:BH * D].rearrange("p (b d) -> p b d", d=D)
        HALF = [slice(h * HI, (h + 1) * HI) for h in range(2)]

        @block.gpsimd
        def _(pool):
            nc.gpsimd.memset(minus_half[:, :], -0.5).then_inc(consts_set, 1)
            pool.wait_ge(consts_set, 1)

            def ln_rstd(b):
                pool.wait_ge(var_ready, b + 1)
                nc.gpsimd.tensor_tensor(rstd, var_eps, minus_half[:, 0:TQ], ALU.pow).then_inc(rstd_ready, 1)

            def squares_and_beta(b, p):
                pool.wait_ge(kq_staged, b * 2 + 2)
                pool.wait_ge(beta_tanh, b + 1)
                nc.gpsimd.tensor_tensor(
                    kn_st[:, bass.ds(b, TQ, B)].rearrange("p q n j -> p q (n j)"),
                    kq_st[:, bass.ds(b, TQ, B), 0:NB * N], kq_st[:, bass.ds(b, TQ, B), 0:NB * N], ALU.mult
                    ).then_inc(ksq_ready, 1)
                nc.gpsimd.tensor_scalar(beta_st[:, p], beta_th[:, p], 0.5, 0.5, ALU.mult, ALU.add
                                        ).then_inc(beta_staged, 1)

            for b in range(3):
                ln_rstd(b)
            for tile in (v_all, beta_all, r_all):
                nc.gpsimd.memset(tile[:, :, T:], 0.0).then_inc(padded, 1)
            with pool.Fori(0, PAIRS - 2) as pair:
                for p in range(2):
                    ln_rstd(pair * 2 + (p + 3))
                    squares_and_beta(pair * 2 + p, p)
            for b in range(B - 4, B):
                if b + 3 < B:
                    ln_rstd(b + 3)
                squares_and_beta(b, b % 2)

            for p in range(2):
                pool.wait_ge(v_stored[p], 16 * PAIRS)
                pool.wait_ge(beta_stored[p], 16 * PAIRS)
            pool.wait_ge(r_ready, 3)
            pool.wait_ge(padded, 3)
            pool.wait_ge(state0, 1)

            def refill(part, t0, half):
                sl = slice(half * GR, (half + 1) * GR)
                if part == 0:
                    nc.gpsimd.tensor_copy(Pk[:, sl, :, N].rearrange("p t i -> p i t"), v_all[:, :, bass.ds(t0, GR)])
                if part == 1:
                    nc.gpsimd.tensor_copy(beta_ring[:, :, sl], beta_all[:, :, bass.ds(t0, GR)])
                if part == 2:
                    nc.gpsimd.tensor_copy(w_ring[:, :, sl], r_all[:, 0:2, bass.ds(t0, GR)]).then_inc(filled[half], 1)

            def state_q(slot, v):
                pool.wait_ge(blended[1], v)
                nc.gpsimd.tensor_tensor(
                    Pq[slot // GR][:, :, slot % GR, :].rearrange("p j i -> p i j"), S[:, slot % SR],
                    q_ring[:, slot].unsqueeze(1).to_broadcast([P, NI, N]), ALU.mult).then_inc(q_used, 1)

            def decay(h, s, v):
                pool.wait_ge(blended[h], v)
                nc.gpsimd.tensor_tensor(bS[:, HALF[h]], S[:, (s - 1) % SR, HALF[h]],
                                        beta_ring[:, HALF[h], s].unsqueeze(2).to_broadcast([P, HI, N]),
                                        ALU.mult).then_inc(bS_ready[h], 1)

            def pool_between(s, k):
                if 1 <= s < 4 and some(k):
                    refill(s - 1, k * CH + GR, 1)
                if s in (GR + 1, GR + 3, GR + 5):
                    refill((s - GR - 1) // 2, k * CH + CH, 0)
                if s == 8:
                    if some(k):
                        pool.wait_ge(bo_ready[1], k)
                    nc.gpsimd.tensor_copy(sm_ring, r_all[:, 2, bass.ds(k * CH, CH)]).then_inc(sm_ready, 1)
                if s == 20 and some(k):
                    residual(k)
                for at, n, c in ((18, 0, k), (23, 1, k), (25, 2, k - 1)):
                    if s == at and some(c):
                        inv_sqrt(n, c)
                if s - 2 in GATE_STEPS and some(k):
                    up_product(GATE_STEPS.index(s - 2), k)
                if s == 29 and some(k - 1):
                    result(k - 1)

            def pool_steps(k):
                for s in range(CH):
                    v = k * CH + (s + 1)
                    if s % GR == 0:
                        pool.wait_ge(filled[s // GR], k + 1)
                    if s == GR // 2 and not some(k):
                        pool.wait_ge(kq_stored, 2 * 16 * TQ)
                    decay(0, s, v)
                    pool_between(s, k)
                    decay(1, s, v)
                    if s % GR == 1:
                        if some(k):
                            pool.wait_ge(sq_psum[s // GR], k)
                        pool.wait_ge(ring_in[s // GR], (k + 1) * RING_LOADS)
                    if s or some(k):
                        state_q((s - 1) % CH, v)

            def inv_sqrt(n, c):
                pool.wait_ge(cvar_ready[n], c)
                nc.gpsimd.tensor_tensor(crs[:, n], cve[:, n], minus_half[:, 0:BH], ALU.pow).then_inc(scale_ready[n], 1)
                pool.wait_ge(scale_ready[n], c)
                nc.gpsimd.tensor_tensor(shift[:, n], minus_mean[:, n], crs[:, n], ALU.mult).then_inc(crs_ready[n], 1)

            def residual(c):
                pool.wait_ge(yn_ready, c)
                pool.wait_ge(xt_in, c * CHUNK_DMAS)
                if some(c - 1):
                    pool.wait_ge(x1_saved, c - 1)
                nc.gpsimd.tensor_tensor(x1, xt, yn, ALU.add).then_inc(x1_ready, 1)

            def result(c):
                pool.wait_ge(on_ready, c)
                if some(c - 1):
                    pool.wait_ge(out_stored, (c - 1) * CHUNK_DMAS)
                pool.wait_ge(x1_saved, c)
                nc.gpsimd.tensor_tensor(o_st, x1_old, on, ALU.add).then_inc(o_staged, 1)

            def up_product(m, c):
                pool.wait_ge(gate_ready[m], c)
                pool.wait_ge(up_ready[m], c)
                nc.gpsimd.tensor_tensor(u[:, m], gate_t[:, m % 2], up[:, m % 2], ALU.mult).then_inc(u_ready[m], 1)

            for half in range(2):
                for part in range(3):
                    refill(part, half * GR, half)
            pool_steps(0)
            pool_steps(1)
            with pool.Fori(2, NC) as k:
                pool_steps(k)
            state_q(CH - 1, T + 1)
            inv_sqrt(0, NC)
            residual(NC)
            inv_sqrt(1, NC)
            inv_sqrt(2, NC - 1)
            for m in range(MH):
                up_product(m, NC)
            result(NC - 1)
            inv_sqrt(2, NC)
            result(NC)

        @block.scalar
        def _(act):
            def copy_xnT(b):
                act.wait_ge(xnT_psum, b + 1)
                nc.scalar.activation(xnT, PS[:, 0, :], ACT.Copy).then_inc(xnT_ready, 1)

            def silu_tanh(b):
                act.wait_ge(xp_psum, b + 1)
                nc.scalar.activation(sg, PS[:, 1, :], ACT.Tanh, scale=0.5).then_inc(sg_ready, 1)

            def stage_v(b, p, pair):
                act.wait_ge(v_psum, b + 1)
                if some(pair):
                    act.wait_ge(v_stored[p], pair * 16)
                nc.scalar.activation(v_st[:, p], PS[:, 2, :], ACT.Copy, scale=-0.5).then_inc(v_staged, 1)

            def stage_kq_beta(b, p, pair):
                act.wait_ge(weights_in, PROJ_WEIGHTS)
                act.wait_ge(kq_psum, b + 1)
                for k in range(2):
                    nc.scalar.activation(kq_st[:, bass.ds(b + 2 * k * B, 2, B), :],
                                         PS[:, 4 + k, 0:2 * KQ].rearrange("p (q c) -> p q c", q=2),
                                         ACT.Copy, scale=0.5).then_inc(kq_staged, 1)
                act.wait_ge(beta_psum, b + 1)
                if some(pair):
                    act.wait_ge(beta_stored[p], pair * 16)
                nc.scalar.activation(beta_th[:, p], PS[:, 3, :], ACT.Tanh, bias=bb_half[:, 0:1], scale=0.25
                                     ).then_inc(beta_tanh, 1)

            def act_project(b, p, pair):
                silu_tanh(b)
                if some(b):
                    before = (b - 1, 1 - p, pair - 1 + p)
                    stage_v(*before)
                if not isinstance(b, int) or b < B - 1:
                    copy_xnT(b + 1)
                if some(b):
                    stage_kq_beta(*before)

            copy_xnT(0)
            act.wait_ge(bb_ready, 1)
            for p in range(2):
                act_project(p, p, 0)
            act_project(2, 0, 1)
            with act.Fori(1, PAIRS - 1) as pair:
                act_project(pair * 2 + 1, 1, pair)
                act_project(pair * 2 + 2, 0, pair + 1)
            act_project(B - 1, 1, PAIRS - 1)
            stage_v(B - 1, 1, PAIRS - 1)
            stage_kq_beta(B - 1, 1, PAIRS - 1)
            act.wait_ge(ld_ready, 1)
            nc.scalar.activation(lexp, ld, ACT.Exp).then_inc(lexp_ready, 1)
            act.wait_ge(ss_ready, 1)
            nc.scalar.activation(nrm, ss, ACT.Sqrt).then_inc(nrm_ready, 1)
            act.wait_ge(soft_ready, 1)
            nc.scalar.activation(r_tok[:, 2].rearrange("p (t n) g -> p t n g", n=NB),
                                 soft.unsqueeze(3).to_broadcast([P, QB, NB, IG]), ACT.Copy
                                 ).then_inc(soft_spread, 1)
            for k in range(3):
                act.wait_ge(r_psum, k + 1)
                nc.scalar.activation(r_all[:, k, 0:T], PS[:, k, :], ACT.Copy, scale=0.5 if k == 2 else 1.0
                                     ).then_inc(r_ready, 1)

            act.wait_ge(state0, 1)

            def keep(h, s, v):
                act.wait_ge(blended[h], v)
                nc.scalar.activation(G[:, HALF[h]], S[:, (s - 1) % SR, HALF[h]], ACT.Copy,
                                     scale=w_ring[:, 1, s:s + 1]).then_inc(G_ready[h], 1)

            def squash(h, v):
                act.wait_ge(pre_ready[h], v)
                nc.scalar.activation(U[:, HALF[h]], pre[:, HALF[h]], ACT.Tanh).then_inc(U_ready[h], 1)

            def sq_tanh_of(half, c):
                act.wait_ge(sq_psum[half], c)
                nc.scalar.activation(sq_th.rearrange("p t i -> p (t i)"), PS[:, half, 0:GR * NI], ACT.Tanh, scale=0.5)
                nc.scalar.activation(sq_a.rearrange("p t i -> p (t i)"), PS[:, half, 0:GR * NI], ACT.Square
                                     ).then_inc(sq_a_ready[half], 1)

            def norm_apply(n, dst, src, ready, c):
                act.wait_ge(crs_ready[n], c)
                for bh in range(BH):
                    ins = nc.scalar.activation(dst[:, bh], src[:, bh], ACT.Identity, bias=shift[:, n, bh:bh + 1],
                                               scale=crs[:, n, bh:bh + 1])
                ins.then_inc(ready, 1)

            def spread_bo(b, c):
                if b == 0:
                    for half in range(2):
                        act.wait_ge(bo_ready[half], c)
                ins = nc.scalar.activation(bo_own[:, :, b], bo, ACT.Copy, scale=own_seq[:, b:b + 1])
                if b == B - 1:
                    ins.then_inc(bo_spread, 1)

            def copy_x1nT(c):
                act.wait_ge(x1nT_psum, c)
                nc.scalar.activation(x1nT, PS[:, 2, 0:TK], ACT.Copy).then_inc(x1nT_ready, 1)

            def save_x1(c):
                act.wait_ge(x1_ready, c)
                if some(c - 1):
                    act.wait_ge(o_staged, c - 1)
                nc.scalar.activation(x1_old, x1, ACT.Copy).then_inc(x1_saved, 1)

            def gate(m, c):
                act.wait_ge(gate_psum[m], c)
                nc.scalar.activation(gate_th[:, m % 2], PS[:, 4 + m % 2, 0:TK], ACT.Tanh,
                                     scale=s1_half[:, m:m + 1]).then_inc(gate_tanh[m], 1)
                nc.scalar.activation(up[:, m % 2], PS[:, 6 + m % 2, 0:TK], ACT.Copy).then_inc(up_ready[m], 1)

            def gelu(dst, psum, ready, scale, m, c):
                act.wait_ge(psum[m], c)
                nc.scalar.activation(dst[:, m], PS[:, 4 + m, 0:TK], ACT.Gelu, scale=scale[:, m:m + 1]
                                     ).then_inc(ready[m], 1)

            def act_between(s, k, c1, c2):
                if some(c2):
                    if 6 <= s < 6 + MH:
                        gelu(g1, h1_psum, g1_ready, sh1, s - 6, c2)
                    if s == 12:
                        save_x1(c2)
                    if 14 <= s < 14 + MH:
                        gelu(g2, h2_psum, g2_ready, sh2, s - 14, c2)
                    if s == 27:
                        norm_apply(2, on, psO, on_ready, c2)
                if some(c1):
                    if s == 5:
                        sq_tanh_of(1, c1)
                    if 8 <= s < 8 + B // 2:
                        for b in range(2):
                            spread_bo((s - 8) * 2 + b, c1)
                    if s == 18:
                        norm_apply(0, yn, psY, yn_ready, c1)
                    if s == 23:
                        norm_apply(1, x1n, x1, x1n_ready, c1)
                    if s == 24:
                        copy_x1nT(c1)
                    if s in GATE_STEPS:
                        gate(GATE_STEPS.index(s), c1)
                if s == 22:
                    sq_tanh_of(0, k + 1)

            def act_steps(k, c1, c2):
                for s in range(CH):
                    v = k * CH + (s + 1)
                    if s % GR == 0:
                        act.wait_ge(filled[s // GR], k + 1)
                    keep(0, s, v)
                    if s or some(k):
                        squash(1, v - 1)
                    squash(0, v)
                    keep(1, s, v)
                    act_between(s, k, c1, c2)

            act.wait_ge(scaled, 1)
            nc.scalar.activation(warm[:, :], s1[:, 0:1], ACT.Gelu)
            act_steps(0, 0, 0)
            act_steps(1, 1, 0)
            with act.Fori(2, NC) as k:
                act_steps(k, k, k - 1)
            squash(1, T)
            save_x1(NC - 1)
            sq_tanh_of(1, NC)
            for b in range(B):
                spread_bo(b, NC)
            for m in range(MH):
                gelu(g1, h1_psum, g1_ready, sh1, m, NC - 1)
            norm_apply(0, yn, psY, yn_ready, NC)
            norm_apply(1, x1n, x1, x1n_ready, NC)
            for m in range(MH):
                gelu(g2, h2_psum, g2_ready, sh2, m, NC - 1)
            copy_x1nT(NC)
            for m in range(MH):
                gate(m, NC)
            norm_apply(2, on, psO, on_ready, NC - 1)
            for m in range(MH):
                gelu(g1, h1_psum, g1_ready, sh1, m, NC)
            save_x1(NC)
            for m in range(MH):
                gelu(g2, h2_psum, g2_ready, sh2, m, NC)
            norm_apply(2, on, psO, on_ready, NC)

        @block.vector
        def _(dve):
            def norm_variance(b, p, pair):
                dve.wait_ge(x_loaded[p], pair * 16 + 16)
                for q in range(TQ):
                    last = nc.vector.bn_stats(ln_stat[:, q], x_in[:, p, q])
                last.then_inc(ln_stats, 1)
                dve.wait_ge(ln_stats, b + 1)
                nc.vector.memset(spacer[:, :], 0.0)
                for q in range(TQ):
                    last = nc.vector.bn_aggr(mv[:, p, q], ln_stat[:, q])
                last.then_inc(ln_aggr, 1)
                dve.wait_ge(ln_aggr, b + 1)
                nc.vector.tensor_scalar(var_eps, mv[:, p, :, 1], EPS, None, ALU.add).then_inc(var_ready, 1)

            def normalize(b, p):
                dve.wait_ge(rstd_ready, b + 1)
                for q in range(TQ):
                    last = nc.vector.tensor_scalar(xn[:, p, q], x_in[:, p, q], mv[:, p, q, 0:1], rstd[:, q:q + 1],
                                                   ALU.subtract, ALU.mult)
                last.then_inc(xn_ready, 1)

            def silu(b, p):
                dve.wait_ge(sg_ready, b + 1)
                nc.vector.scalar_tensor_tensor(out=xpT[:, p], in0=sg, scalar=1.0, in1=PS[:, 1, :], op0=ALU.add,
                                               op1=ALU.mult).then_inc(xp_ready, 1)

            norm_variance(0, 0, 0)
            normalize(0, 0)
            norm_variance(1, 1, 0)
            dve.wait_ge(weights_in, PROJ_WEIGHTS)
            nc.vector.tensor_scalar(bb_half[:, :], bb[:, :], 0.5, None, ALU.mult).then_inc(bb_ready, 1)
            with dve.Fori(0, PAIRS - 1) as pair:
                for p in range(2):
                    normalize(pair * 2 + (p + 1), 1 - p)
                    silu(pair * 2 + p, p)
                    norm_variance(pair * 2 + (p + 2), p, pair + 1)
            normalize(B - 1, 1)
            silu(B - 2, 0)
            silu(B - 1, 1)

            chained = [0]

            def link(ins):
                chained[0] += 1
                ins.then_inc(router, 1)
                dve.wait_ge(router, chained[0])

            dve.wait_ge(kq_staged, 2 * B)
            lg = kq_st[:, :, NB * N + N:]
            link(nc.vector.tensor_reduce(lmax, lg, AX.X, ALU.max))
            nc.vector.tensor_tensor(ld, lg, lmax.unsqueeze(2).to_broadcast([P, QB, NB]), ALU.subtract
                                    ).then_inc(ld_ready, 1)
            for n in range(NB):
                link(nc.vector.memset(wins[:, :, n:n + 1], float(n)))
            for s in range(1, NB):
                link(nc.vector.tensor_tensor(ge[:, :, 0:NB - s], lg[:, :, 0:NB - s], lg[:, :, s:NB], ALU.is_ge))
                link(nc.vector.tensor_tensor(wins[:, :, 0:NB - s], wins[:, :, 0:NB - s], ge[:, :, 0:NB - s],
                                             ALU.add))
                link(nc.vector.tensor_tensor(wins[:, :, s:NB], wins[:, :, s:NB], ge[:, :, 0:NB - s],
                                             ALU.subtract))
            link(nc.vector.tensor_scalar(mask, wins, float(NB - 2), None, ALU.is_ge))
            dve.wait_ge(ksq_ready, B)
            nc.vector.tensor_reduce(ss, kn_st.rearrange("p q n j -> p (q n) j"), AX.X, ALU.add
                                    ).then_inc(ss_ready, 1)
            dve.wait_ge(lexp_ready, 1)
            link(nc.vector.tensor_reduce(lsum, lexp, AX.X, ALU.add))
            link(nc.vector.reciprocal(lsrec, lsum))
            nc.vector.tensor_tensor(soft, lexp, lsrec.unsqueeze(2).to_broadcast([P, QB, NB]), ALU.mult
                                    ).then_inc(soft_ready, 1)
            dve.wait_ge(soft_ready, 1)
            link(nc.vector.tensor_tensor(uw, mask, soft, ALU.mult))
            link(nc.vector.tensor_reduce(usum, uw, AX.X, ALU.add))
            link(nc.vector.tensor_scalar(usum_e, usum, 1e-8, None, ALU.add))
            link(nc.vector.reciprocal(urec, usum_e))
            link(nc.vector.tensor_tensor(
                r_tok[:, 0].rearrange("p (t n) g -> p t n g", n=NB), uw.unsqueeze(3).to_broadcast([P, QB, NB, IG]),
                urec.unsqueeze(2).unsqueeze(3).to_broadcast([P, QB, NB, IG]), ALU.mult))
            nc.vector.tensor_scalar(r_tok[:, 1], r_tok[:, 0], -1.0, 1.0, ALU.mult, ALU.add).then_inc(r_tok_ready, 1)
            dve.wait_ge(nrm_ready, 1)
            link(nc.vector.tensor_scalar(nrm_eps, nrm, 1e-6, None, ALU.add))
            link(nc.vector.reciprocal(rnrm, nrm_eps))
            for q in range(TQ):
                tiles = slice(q * B, (q + 1) * B)
                nc.vector.tensor_tensor(
                    kn_st[:, tiles].rearrange("p b n j -> p (b n) j"),
                    kq_st[:, tiles, 0:NB * N].rearrange("p b (n j) -> p b n j", j=N),
                    rnrm[:, q * B * NB:(q + 1) * B * NB].rearrange("p (b n) -> p b n", n=NB).unsqueeze(3)
                    .to_broadcast([P, B, NB, N]), ALU.mult).then_inc(kn_staged, 1)

            dve.wait_ge(ffn_weights_in, FFN_WEIGHTS)
            nc.vector.tensor_scalar(s1_half[:, :], s1[:, :], 0.5, None, ALU.mult).then_inc(setup, 1)
            dve.wait_ge(setup, 1)
            nc.vector.tensor_tensor(s12[:, :], s1_half[:, :], s2[:, :], ALU.mult).then_inc(setup, 1)
            dve.wait_ge(setup, 2)
            for m in range(MH):
                nc.vector.tensor_scalar(h1[:, m], h1[:, m], s12[:, m:m + 1], None, ALU.mult)
                last = nc.vector.tensor_tensor(w3[:, m], w3[:, m], s3[:, :], ALU.mult)
            last.then_inc(scaled, 1)

            for p in range(2):
                dve.wait_ge(v_stored[p], 16 * PAIRS)
                dve.wait_ge(beta_stored[p], 16 * PAIRS)
            dve.wait_ge(r_psum, 3)
            nc.vector.memset(spacer[:, :], 0.0).then_inc(state0, 1)
            for h in range(2):
                nc.vector.memset(S[:, :, HALF[h]], 0.0).then_inc(blended[h], 1)
            nc.vector.memset(outer, 0.0).then_inc(q_used, SR)

            def product(h, s, v):
                dve.wait_ge(blended[h], v)
                nc.vector.tensor_tensor(Pk[:, s, HALF[h], 0:N], S[:, (s - 1) % SR, HALF[h]],
                                        kn_ring[:, s].unsqueeze(1).to_broadcast([P, HI, N]), ALU.mult
                                        ).then_inc(Pk_ready[h], 1)

            def retrieve(h, s, v):
                dve.wait_ge(Pk_ready[h], v)
                nc.vector.tensor_reduce(delta[:, HALF[h]], Pk[:, s, HALF[h]], AX.X, ALU.add, negate=True
                                        ).then_inc(delta_ready[h], 1)

            def outer_product(h, s, v):
                dve.wait_ge(delta_ready[h], v)
                nc.vector.tensor_tensor(outer[:, HALF[h]], delta[:, HALF[h]].unsqueeze(2).to_broadcast([P, HI, N]),
                                        kn_ring[:, s].unsqueeze(1).to_broadcast([P, HI, N]), ALU.mult
                                        ).then_inc(outer_ready[h], 1)

            def add_decayed(h, v):
                dve.wait_ge(outer_ready[h], v)
                dve.wait_ge(bS_ready[h], v)
                nc.vector.tensor_tensor(pre[:, HALF[h]], outer[:, HALF[h]], bS[:, HALF[h]], ALU.add
                                        ).then_inc(pre_ready[h], 1)

            def blend(h, s, v):
                dve.wait_ge(U_ready[h], v)
                dve.wait_ge(G_ready[h], v)
                if h == 0:
                    dve.wait_ge(q_used, v)
                nc.vector.scalar_tensor_tensor(out=S[:, s % SR, HALF[h]], in0=U[:, HALF[h]],
                                               scalar=w_ring[:, 0, s:s + 1], in1=G[:, HALF[h]],
                                               op0=ALU.mult, op1=ALU.add).then_inc(blended[h], 1)

            def readout(n, half, c):
                if n == 0:
                    dve.wait_ge(sq_a_ready[half], c)
                    nc.vector.scalar_tensor_tensor(out=sq_b, in0=sq_th, scalar=1.0, in1=sq_a, op0=ALU.add, op1=ALU.mult
                                                   ).then_inc(sq_b_ready[half], 1)
                if n == 1:
                    if half == 0:
                        dve.wait_ge(sm_ready, c)
                    dve.wait_ge(sq_b_ready[half], c)
                    nc.vector.tensor_tensor(bo[:, :, half * GR:(half + 1) * GR].rearrange("p i t -> p t i"), sq_b,
                                            sm_ring[:, half * GR:(half + 1) * GR].unsqueeze(2)
                                            .to_broadcast([P, GR, NI]), ALU.mult).then_inc(bo_ready[half], 1)

            def norm_stats(n, src, bh, ready, c):
                if bh == 0:
                    dve.wait_ge(ready, c)
                ins = nc.vector.bn_stats(cst[:, n, bh], src[:, bh])
                if bh == BH - 1:
                    ins.then_inc(stats_ready[n], 1)

            def norm_aggr(n, c):
                dve.wait_ge(stats_ready[n], c)
                nc.vector.memset(spacer[:, :], 0.0)
                for bh in range(BH):
                    last = nc.vector.bn_aggr(cmv[:, n, bh], cst[:, n, bh])
                last.then_inc(aggr_ready[n], 1)

            def norm_var(n, c):
                dve.wait_ge(aggr_ready[n], c)
                nc.vector.tensor_scalar(minus_mean[:, n], cmv[:, n, :, 0], -1.0, None, ALU.mult)
                nc.vector.tensor_scalar(cve[:, n], cmv[:, n, :, 1], EPS, None, ALU.add).then_inc(cvar_ready[n], 1)

            def gate_product(m, c):
                dve.wait_ge(gate_tanh[m], c)
                nc.vector.scalar_tensor_tensor(out=gate_t[:, m % 2], in0=gate_th[:, m % 2], scalar=1.0,
                                               in1=PS[:, 4 + m % 2, 0:TK], op0=ALU.add, op1=ALU.mult
                                               ).then_inc(gate_ready[m], 1)

            def dve_between(s, slot, k, c1, c2):
                at = (s, slot)
                if some(c1):
                    if at in ((6, 1), (7, 0)):
                        readout(1 - slot, 1, c1)
                    if at in ((15, 0), (15, 1)):
                        norm_stats(0, psY, slot, y_psum, c1)
                    if at == (16, 0):
                        norm_aggr(0, c1)
                    if at == (16, 1):
                        norm_var(0, c1)
                    if at in ((20, 1), (21, 0)):
                        norm_stats(1, x1, 1 - slot, x1_ready, c1)
                    if at == (21, 1):
                        norm_aggr(1, c1)
                    if at == (22, 0):
                        norm_var(1, c1)
                    if s - 1 in GATE_STEPS and slot == 0:
                        gate_product(GATE_STEPS.index(s - 1), c1)
                if some(c2):
                    if at in ((22, 1), (23, 0)):
                        norm_stats(2, psO, 1 - slot, o_psum, c2)
                    if at == (23, 1):
                        norm_aggr(2, c2)
                    if at == (24, 0):
                        norm_var(2, c2)
                if at in ((24, 1), (25, 0)):
                    readout(1 - slot, 0, k + 1)

            def dve_steps(k, c1, c2):
                for s in range(CH):
                    first = not some(k) and s == 0
                    v = k * CH + (s + 1)
                    before = (s - 1) % CH
                    if s % GR == 0:
                        dve.wait_ge(filled[s // GR], k + 1)
                        dve.wait_ge(ring_in[s // GR], (k + 1) * RING_LOADS)
                    product(0, s, v)
                    if not first:
                        outer_product(1, before, v - 1)
                    retrieve(0, s, v)
                    if not first:
                        add_decayed(1, v - 1)
                    outer_product(0, s, v)
                    dve_between(s, 0, k, c1, c2)
                    add_decayed(0, v)
                    if not first:
                        blend(1, before, v - 1)
                    dve_between(s, 1, k, c1, c2)
                    product(1, s, v)
                    blend(0, s, v)
                    retrieve(1, s, v)

            dve_steps(0, 0, 0)
            dve_steps(1, 1, 0)
            with dve.Fori(2, NC) as k:
                dve_steps(k, k, k - 1)
            outer_product(1, CH - 1, T)
            add_decayed(1, T)
            blend(1, CH - 1, T)
            def last_norm(n, src, ready, c):
                for bh in range(BH):
                    norm_stats(n, src, bh, ready, c)
                norm_aggr(n, c)
                norm_var(n, c)

            for n in range(2):
                readout(n, 1, NC)
            last_norm(0, psY, y_psum, NC)
            last_norm(1, x1, x1_ready, NC)
            last_norm(2, psO, o_psum, NC - 1)
            for m in range(MH):
                gate_product(m, NC)
            last_norm(2, psO, o_psum, NC)

        @block.tensor
        def _(pe):
            def transpose_xn(b, p):
                pe.wait_ge(xn_ready, b + 1)
                for q in range(TQ):
                    last = nc.tensor.transpose(PS[:, 0, q * P:(q + 1) * P], xn[:, p, q], ident[:, :])
                last.then_inc(xnT_psum, 1)

            def project_in(b):
                pe.wait_ge(xnT_ready, b + 1)
                if some(b):
                    pe.wait_ge(xp_ready, b)
                nc.tensor.matmul(PS[:, 1, :], w_in[:, :], xnT, start=True, stop=True).then_inc(xp_psum, 1)

            def project_v(p):
                nc.tensor.matmul(PS[:, 2, :], w_v[:, :], xpT[:, p], start=True, stop=True).then_inc(v_psum, 1)

            def project_kq_beta(p):
                for q in range(TQ):
                    last = nc.tensor.matmul(PS[:, 4 + q // 2, (q % 2) * KQ:(q % 2 + 1) * KQ],
                                            xpT[:, p, q * P:(q + 1) * P], w_kqr[:, :], start=(q % 2 == 0),
                                            stop=True, skip_group_check=True)
                last.then_inc(kq_psum, 1)
                nc.tensor.matmul(PS[:, 3, :], w_beta[:, :], xpT[:, p], start=True, stop=True
                                 ).then_inc(beta_psum, 1)

            def pe_project(b, p):
                project_in(b)
                if some(b):
                    project_v(1 - p)
                if not isinstance(b, int) or b < B - 1:
                    transpose_xn(b + 1, 1 - p)
                if some(b):
                    pe.wait_ge(sg_ready, b + 1)
                    project_kq_beta(1 - p)

            pe.wait_ge(weights_in, PROJ_WEIGHTS)
            transpose_xn(0, 0)
            for p in range(2):
                pe_project(p, p)
            with pe.Fori(1, PAIRS - 1) as pair:
                for p in range(2):
                    pe_project(pair * 2 + p, p)
            for p in range(2):
                pe_project(B - 2 + p, p)
            pe.wait_ge(xp_ready, B)
            pe.wait_ge(v_staged, B - 1)
            project_v(1)
            pe.wait_ge(beta_tanh, B - 1)
            project_kq_beta(1)
            pe.wait_ge(r_tok_ready, 1)
            pe.wait_ge(v_staged, B)
            pe.wait_ge(soft_spread, 1)
            for k in range(3):
                for q in range(TQ):
                    last = nc.tensor.matmul(PS[:, k, q * P:(q + 1) * P],
                                            r_tok[:, k, q * B * NB:(q + 1) * B * NB].rearrange("p c g -> p (c g)"),
                                            ident[:, :], start=(q == 0), stop=True, skip_group_check=True)
                last.then_inc(r_psum, 1)

            pe.wait_ge(scaled, 1)

            def sum_q(half, k):
                pe.wait_ge(q_used, k * CH + (half + 1) * GR + SR)
                if some(k):
                    pe.wait_ge(bo_ready[half], k)
                for j in range(N):
                    last = nc.tensor.matmul(PS[:, half, 0:GR * NI], ident[:, :],
                                            Pq[half][:, j].rearrange("p t i -> p (t i)"),
                                            start=(j == 0), stop=(j == N - 1))
                last.then_inc(sq_psum[half], 1)

            def project(c):
                pe.wait_ge(bo_spread, c)
                for bh in range(BH):
                    for i in range(NI):
                        last = nc.tensor.matmul(PS[:, 2, bh * D:(bh + 1) * D],
                                                bo_own[:, i, 4 * bh:4 * bh + 4].rearrange("p b t -> p (b t)"),
                                                w_out[:, i], start=(i == 0), stop=(i == NI - 1),
                                                skip_group_check=True)
                last.then_inc(y_psum, 1)

            def transpose_x1n(c):
                pe.wait_ge(x1n_ready, c)
                for bh in range(BH):
                    last = nc.tensor.transpose(PS[:, 2, bh * P:(bh + 1) * P], x1n[:, bh], ident[:, :])
                last.then_inc(x1nT_psum, 1)

            def gate_up(c):
                pe.wait_ge(x1nT_ready, c)
                for m in range(MH):
                    if m >= 2:
                        pe.wait_ge(u_ready[m - 2], c)
                    nc.tensor.matmul(PS[:, 6 + m % 2, 0:TK], w2[:, m * P:(m + 1) * P], x1nT, start=True, stop=True)
                    nc.tensor.matmul(PS[:, 4 + m % 2, 0:TK], w1[:, m * P:(m + 1) * P], x1nT, start=True, stop=True
                                     ).then_inc(gate_psum[m], 1)

            def hidden(w, src, src_ready, psum, c):
                for k in range(MH):
                    pe.wait_ge(src_ready[k], c)
                for m in range(MH):
                    for k in range(MH):
                        last = nc.tensor.matmul(PS[:, 4 + m, 0:TK], w[:, k, m * P:(m + 1) * P], src[:, k],
                                                start=(k == 0), stop=(k == MH - 1))
                    last.then_inc(psum[m], 1)

            def down(c):
                for k in range(MH):
                    pe.wait_ge(g2_ready[k], c)
                for bh in range(BH):
                    for k in range(MH):
                        last = nc.tensor.matmul(PS[:, 3, bh * D:(bh + 1) * D], g2[:, k, bh * P:(bh + 1) * P], w3[:, k],
                                                start=(k == 0), stop=(k == MH - 1), skip_group_check=True)
                last.then_inc(o_psum, 1)

            def pe_turn(k, c1, c2):
                if some(c1):
                    sum_q(1, k - 1)
                if some(c2):
                    hidden(h1, u, u_ready, h1_psum, c2)
                if some(c2):
                    hidden(h2, g1, g1_ready, h2_psum, c2)
                if some(c1):
                    project(c1)
                if some(c2):
                    down(c2)
                sum_q(0, k)
                if some(c1):
                    transpose_x1n(c1)
                    gate_up(c1)

            pe_turn(0, 0, 0)
            pe_turn(1, 1, 0)
            with pe.Fori(2, NC) as k:
                pe_turn(k, k, k - 1)
            sum_q(1, NC - 1)
            hidden(h1, u, u_ready, h1_psum, NC - 1)
            project(NC)
            hidden(h2, g1, g1_ready, h2_psum, NC - 1)
            down(NC - 1)
            transpose_x1n(NC)
            gate_up(NC)
            hidden(h1, u, u_ready, h1_psum, NC)
            hidden(h2, g1, g1_ready, h2_psum, NC)
            down(NC)


def kernel(L0_attn_x, L0_attn_W_in, L0_attn_W_router, L0_attn_W_kv, L0_attn_W_beta, L0_attn_b_beta,
           L0_attn_W_q, L0_attn_W_out, L0_ffn_w1_w, L0_ffn_w1_s, L0_ffn_w2_w, L0_ffn_w2_s, L0_ffn_h1_w,
           L0_ffn_h1_s, L0_ffn_h2_w, L0_ffn_h2_s, L0_ffn_w3_w, L0_ffn_w3_s):
    import numpy as np
    import concourse.bacc as bacc
    from concourse.bass_utils import run_bass_kernel_spmd

    B, _, D = L0_attn_x.shape
    NB, N = L0_attn_b_beta.shape
    IG = 4
    kv = np.asarray(L0_attn_W_kv).reshape(NB, 2, N, D)
    W_k = kv[:, 0].reshape(NB * N, D)
    W_v = kv[:, 1].reshape(NB * N, D)

    def column(s):
        return np.asarray(s).reshape(-1, 128).T

    W_out_rows = np.asarray(L0_attn_W_out).T.reshape(IG, (N // IG) * D)
    arrays = {
        "x": L0_attn_x,
        "W_inT": np.asarray(L0_attn_W_in).T,
        "W_kqrT": np.concatenate([W_k, np.asarray(L0_attn_W_q), np.asarray(L0_attn_W_router)]).T,
        "W_vT": W_v.T,
        "W_betaT": np.asarray(L0_attn_W_beta).T,
        "b_beta": np.asarray(L0_attn_b_beta).reshape(NB * N, 1),
        "W_out_rows": np.tile(W_out_rows, (B * NB, 1)),
        "w1T": np.asarray(L0_ffn_w1_w).T,
        "w2T": np.asarray(L0_ffn_w2_w).T,
        "h1T": np.asarray(L0_ffn_h1_w).T,
        "h2T": np.asarray(L0_ffn_h2_w).T,
        "w3T": np.asarray(L0_ffn_w3_w).T,
        "w1_s": column(L0_ffn_w1_s),
        "w2_s": column(L0_ffn_w2_s),
        "h1_s": column(L0_ffn_h1_s),
        "h2_s": column(L0_ffn_h2_s),
        "w3_s": np.tile(np.asarray(L0_ffn_w3_s), (128, 1)),
        "ident_in": np.eye(128, dtype=np.float32),
        "own_seq_in": np.repeat(np.eye(B, dtype=np.float32), NB * IG, axis=0),
    }
    nc = bacc.Bacc("TRN2", target_bir_lowering=False, num_devices=1)
    feeds, args = {}, []
    for name, a in arrays.items():
        a = np.ascontiguousarray(a)
        feeds[name + "_dram"] = a
        args.append(nc.dram_tensor(name + "_dram", a.shape, mybir.dt.from_np(a.dtype), kind="ExternalInput").ap())
    args.append(nc.dram_tensor("out_dram", np.asarray(L0_attn_x).shape, F32, kind="ExternalOutput").ap())
    sandwich(nc, *args)
    r = run_bass_kernel_spmd(nc, [feeds], core_ids=[0])
    return r.results[0]["out_dram"]
```
